# Optimizing a Trainium2 kernel written in Bass

```python
import numpy as np
import jax
import jax.numpy as jnp

def _softmax(x, axis=-1):
    return jax.nn.softmax(x, axis=axis)

def _gelu(x):
    return jax.nn.gelu(x, approximate=True)

def _silu(x):
    return jax.nn.silu(x)

def _sigmoid(x):
    return jax.nn.sigmoid(x)

def _layernorm(x, axis=-1, eps=1e-05):
    m = jnp.mean(x, axis=axis, keepdims=True)
    v = jnp.var(x, axis=axis, keepdims=True)
    return (x - m) / jnp.sqrt(v + eps)

def _scatter_add(tgt, idx, src, axis=0):
    return tgt.at[idx].add(src)

def _segment_sum(src, seg, n):
    return jax.ops.segment_sum(src, seg, n)
kernel_name = 'mk_flamingo_gated_d1_seqx_r2_0164e8'

def setup_inputs(seed: int=0):
    np.random.seed(seed)
    _w = jnp.asarray

    def _rec_inputs():
        import jax
        import jax.numpy as jnp
        _rk = jax.random.key(seed)
        x = -0.0003929 + 0.9999 * jax.random.normal(jax.random.fold_in(_rk, 1), (4, 2048, 512), jnp.float32)
        _lenS = 2048 - jax.random.randint(jax.random.fold_in(_rk, 7), (4,), 0, max(1, 2048 // 4) + 1, jnp.int32)
        _lenS2 = 77 - jax.random.randint(jax.random.fold_in(_rk, 8), (4,), 0, max(1, 77 // 4) + 1, jnp.int32)
        _ctx_768P = jax.random.normal(jax.random.fold_in(_rk, 11), (4, 16, 384), jnp.float32)
        _ctx_768c = jax.random.dirichlet(jax.random.fold_in(_rk, 511), 0.3 * jnp.ones((16,), jnp.float32), (4, 77))
        _ctx_768t = jnp.einsum('bsk,bkd->bsd', _ctx_768c, _ctx_768P)
        _ctx_768t = _ctx_768t * jax.lax.rsqrt(jnp.mean(jnp.square(_ctx_768t)) + 1e-12) * 0.953939
        ctx_768 = 2.09791e-05 + 1.00001 * (_ctx_768t + 0.3 * jax.random.normal(jax.random.fold_in(_rk, 611), (4, 77, 384), jnp.float32))
        _g = jax.random.normal(jax.random.fold_in(_rk, 9001), (2, 1), jnp.float32)
        _g = jnp.sign(_g) * jnp.maximum(jnp.abs(_g), 1.0) + (_g == 0) * 1.0
        g_xattn = _g[0]
        g_ffn = _g[1]
        return (x, ctx_768, g_xattn, g_ffn)
    x, ctx_768, g_xattn, g_ffn = _rec_inputs()

    def _L0_xattn_setup():
        import jax, jax.numpy as jnp
        import numpy as np
        HEADS = 16
        DIM_HEAD = 64
        SCALE = DIM_HEAD ** (-0.5)
        key = jax.random.key(seed)
        ks = jax.random.split(key, 7)
        B, SQ, SKV, QD, CD, ID = (4, 2048, 512, 512, 384, HEADS * DIM_HEAD)
        s = lambda d: 1.0 / np.sqrt(d)
        return {'x': jax.random.normal(ks[0], (B, SQ, QD), jnp.float32), 'context': jax.random.normal(ks[1], (B, SKV, CD), jnp.float32), 'Wq': jax.random.normal(ks[2], (QD, ID), jnp.float32) * s(QD), 'Wk': jax.random.normal(ks[3], (CD, ID), jnp.float32) * s(CD), 'Wv': jax.random.normal(ks[4], (CD, ID), jnp.float32) * s(CD), 'Wo': jax.random.normal(ks[5], (ID, QD), jnp.float32) * s(ID), 'bo': jnp.zeros((QD,), jnp.float32)}
    _L0_xattn_all = _L0_xattn_setup()
    _L0_xattn_in = {k: v for k, v in _L0_xattn_all.items() if k in ('Wq', 'Wk', 'Wv', 'Wo', 'bo')}
    del _L0_xattn_all

    def _L0_ffn_setup():
        import jax, jax.numpy as jnp
        import numpy as np
        NUM_OPS, B, T, D = (8, 8, 256, 512)
        key = jax.random.key(seed)
        k1, k2, k3, k4 = jax.random.split(key, 4)
        x = jax.random.normal(k1, (B, T, D), dtype=jnp.float32)
        W = jax.random.normal(k2, (NUM_OPS, D, D), dtype=jnp.float32) * 0.02
        b = jnp.zeros((NUM_OPS, D), dtype=jnp.float32)
        logits = 0.001 * jax.random.normal(k3, (NUM_OPS,), dtype=jnp.float32)
        u = jax.random.uniform(k4, (NUM_OPS,), dtype=jnp.float32, minval=1e-06, maxval=1.0 - 1e-06)
        return {'x': x, 'W': W, 'b': b, 'logits': logits, 'u': u}
    _L0_ffn_all = _L0_ffn_setup()
    _L0_ffn_in = {k: v for k, v in _L0_ffn_all.items() if k in ('W', 'b', 'logits', 'u')}
    del _L0_ffn_all
    return {'x': x, 'ctx_768': ctx_768, 'g_xattn': g_xattn, 'g_ffn': g_ffn, 'L0_xattn_Wq': _L0_xattn_in['Wq'], 'L0_xattn_Wk': _L0_xattn_in['Wk'], 'L0_xattn_Wv': _L0_xattn_in['Wv'], 'L0_xattn_Wo': _L0_xattn_in['Wo'], 'L0_xattn_bo': _L0_xattn_in['bo'], 'L0_ffn_W': _L0_ffn_in['W'], 'L0_ffn_b': _L0_ffn_in['b'], 'L0_ffn_logits': _L0_ffn_in['logits'], 'L0_ffn_u': _L0_ffn_in['u']}

def reference(x, ctx_768, g_xattn, g_ffn, L0_xattn_Wq, L0_xattn_Wk, L0_xattn_Wv, L0_xattn_Wo, L0_xattn_bo, L0_ffn_W, L0_ffn_b, L0_ffn_logits, L0_ffn_u):
    import jax
    import jax.numpy as jnp

    def _L0_xattn_ref(x, context, Wq, Wk, Wv, Wo, bo):
        import jax, jax.numpy as jnp
        import numpy as np
        HEADS = 16
        DIM_HEAD = 64
        SCALE = DIM_HEAD ** (-0.5)
        b, sq, _ = x.shape

        def split_heads(t):
            return t.reshape(b, -1, HEADS, DIM_HEAD).transpose(0, 2, 1, 3)
        q = split_heads(x @ Wq)
        k = split_heads(context @ Wk)
        v = split_heads(context @ Wv)
        sim = jnp.einsum('bhid,bhjd->bhij', q, k) * SCALE
        attn = jax.nn.softmax(sim, axis=-1)
        out = jnp.einsum('bhij,bhjd->bhid', attn, v)
        out = out.transpose(0, 2, 1, 3).reshape(b, sq, HEADS * DIM_HEAD)
        return out @ Wo + bo

    def _L0_ffn_ref(x, W, b, logits, u):
        import jax, jax.numpy as jnp
        import numpy as np
        NUM_OPS, B, T, D = (8, 8, 256, 512)
        gumbel = -jnp.log(-jnp.log(u))
        idx = jnp.argmax(jax.nn.log_softmax(logits) + gumbel)
        out = jnp.einsum('btd,de->bte', x, W[idx]) + b[idx]
        return out
    x = x + jnp.tanh(g_xattn[0]) * _L0_xattn_ref(_layernorm(x, axis=-1), ctx_768, L0_xattn_Wq, L0_xattn_Wk, L0_xattn_Wv, L0_xattn_Wo, L0_xattn_bo)
    x = x + jnp.tanh(g_ffn[0]) * _L0_ffn_ref(_layernorm(x, axis=-1), L0_ffn_W, L0_ffn_b, L0_ffn_logits, L0_ffn_u)
    return x

_drawn_inputs = setup_inputs


def setup_inputs(seed=0):
    import zlib

    import numpy as np

    out = dict(_drawn_inputs(seed))
    spreads = {'L0_xattn_bo': (0.0, 0.1), 'L0_ffn_b': (0.0, 0.1)}
    factors = {}
    for name, (base, spread) in spreads.items():
        noise = np.random.default_rng([zlib.crc32(name.encode()), seed]).standard_normal(out[name].shape)
        drawn = base * np.exp(spread * noise) if base else spread * noise
        out[name] = jnp.asarray(drawn.astype(out[name].dtype))
    for name, factor in factors.items():
        out[name] = (out[name] * factor).astype(out[name].dtype)
    return out
```

```python
from contextlib import ExitStack

import concourse.bass as bass
from concourse import mybir

ALU = mybir.AluOpType
ACT = mybir.ActivationFunctionType
AX = mybir.AxisListType
F32 = mybir.dt.float32
F16 = mybir.dt.float16
U32 = mybir.dt.uint32

P = 128
HEADS = 16
DH = 64
EPS = 1e-5
OPERAND_BITS = 10
FOLD_BITS = -13
XN_BITS = 8
PROB_BITS = 14
WF_BITS = 13


def flamingo_layer(nc, x, ctx_in, g_xattn, g_ffn, wq, wk, wv, wo, bo, ffn_w, ffn_b, logits, u, out):
    B, SQ, D = x.shape
    _, J, CD = ctx_in.shape
    ID = HEADS * DH
    HJ = HEADS * J
    NOPS = ffn_w.shape[0]
    KT = D // P
    CT = CD // P
    HP = ID // P
    BJ = B * J
    NQ = SQ // P
    CHUNKS = [(c, min(c + P, HJ)) for c in range(0, HJ, P)]
    NC = len(CHUNKS)
    GROUPS = [range(0, 4), range(4, 8), range(8, NC)]
    NG = len(GROUPS)
    HB = 512 // J
    BANKS = [(h, min(h + HB, HEADS)) for h in range(0, HEADS, HB)]
    NT = B * NQ
    FIRST = 6
    LOOPS = (NT - 4 - FIRST) // B
    assert B == 4 and D == 512 and len(BANKS) == 3
    FULL = len(BANKS) - 1

    with ExitStack() as stack:
        def sb(name, shape, dt=F32):
            return stack.enter_context(nc.sbuf_tensor(name, shape, dt))

        def sem(name):
            return stack.enter_context(nc.semaphore(name))

        a_split = sb("a_split", [P, 2, KT, B, HJ], F16)
        wf_split = sb("wf_split", [P, 2, KT, D], F16)
        VW_WORDS = B * 2 * NC * D // 2
        vw_arena = sb("vw_arena", [P, VW_WORDS])
        vw = vw_arena[:, :].bitcast(F16).rearrange("p (b s c d) -> p b s c d", b=B, s=2, c=NC)
        LOOP_WORDS = HP * D + B * HJ + 2 * HP * BJ
        arena = sb("arena", [P, LOOP_WORDS])
        ident = sb("ident", [P, P])
        cst = sb("cst", [P, 64])
        stats = sb("stats", [P, 64])
        pick = sb("pick", [1, 80])
        pick_idx = sb("pick_idx", [1, 8], U32)

        class Carve:
            def __init__(self, base):
                self.base, self.at = base, 0

            def take(self, words):
                self.at += words
                return self.base[:, self.at - words:self.at]

        c = Carve(vw_arena)
        wq_raw = c.take(KT * ID).rearrange("p (k n) -> p k n", k=KT)
        wk_raw = c.take(CT * ID).rearrange("p (k n) -> p k n", k=CT)
        wv_raw = c.take(CT * ID).rearrange("p (k n) -> p k n", k=CT)
        wqT = c.take(HP * D).bitcast(F16).rearrange("p (s h n) -> p s h n", s=2, h=HP)
        ctxT = c.take(CT * BJ).rearrange("p (k n) -> p k n", k=CT)
        kvT = c.take(HP * BJ).rearrange("p (h n) -> p h n", h=HP)
        assert c.at <= VW_WORDS, c.at
        c = Carve(arena)
        wo_split = c.take(HP * D).bitcast(F16).rearrange("p (s h n) -> p s h n", s=2, h=HP)
        vwT_words = B * HJ
        at_vwT = c.at
        vwT = c.take(vwT_words).rearrange("p (b n) -> p b n", b=B)
        wo_raw = arena[:, at_vwT:at_vwT + HP * D].rearrange("p (h n) -> p h n", h=HP)
        diag = c.take(2 * HP * 2 * BJ // 2).bitcast(F16).rearrange("p (s h e n) -> p s h e n", s=2, h=HP, e=2)
        assert c.at <= LOOP_WORDS, c.at
        ctx_raw = arena[0:J, 0:B * CD].rearrange("p (b n) -> p b n", b=B)
        wf_raw = arena[:, at_vwT:at_vwT + KT * D].rearrange("p (k n) -> p k n", k=KT)

        c = Carve(arena)
        xin = c.take(4 * D).rearrange("p (r n) -> p r n", r=4)
        res = c.take(4 * D).rearrange("p (r n) -> p r n", r=4)
        outb = c.take(2 * D).rearrange("p (r n) -> p r n", r=2)
        xn = c.take(D)
        xn2 = c.take(D)
        xT = c.take(D).bitcast(F16).rearrange("p (s k n) -> p s k n", s=2, k=KT)
        x2T = c.take(D).bitcast(F16).rearrange("p (s k n) -> p s k n", s=2, k=KT)
        probs = c.take(2 * HJ).rearrange("p (r n) -> p r n", r=2)
        bias = c.take(2 * D).rearrange("p (k n) -> p k n", k=2)
        pT = c.take(NC * P).bitcast(F16).rearrange("p (s c n) -> p s c n", s=2, c=NC)
        assert c.at <= LOOP_WORDS, c.at

        amax, pow2, scl = cst[:, 0:8], cst[:, 8:16], cst[:, 16:24]
        WQ, KK, VV, WO, WF = range(5)
        amax_all = cst[:, 24:32]
        exp_scale, o_scale, f_scale = cst[:, 32:33], cst[:, 33:34], cst[:, 34:35]
        gates, gate_in = cst[:, 36:38], cst[:, 38:40]
        neg_half = cst[:, 40:41]
        eps = cst[:, 41:42]
        bn1, mv1, rstd1, ve1 = stats[:, 0:6], stats[:, 6:8], stats[:, 8:9], stats[:, 9:10]
        bn2, mv2, rstd2, ve2 = stats[:, 12:18], stats[:, 18:20], stats[:, 20:21], stats[:, 21:22]
        mx, sums, rsum = stats[:, 24:40], stats[:, 40:56], cst[:, 44:60]

        banks = stack.enter_context(nc.psum_tensor("banks", [P, 8, 512], F32))
        s_ps = banks[:, 0:3, :]
        pt_ps = [banks[:, 3, :], banks[:, 4, :]]
        o_ps, f_ps, t_ps = banks[:, 5, :], banks[:, 6, :], banks[:, 7, :]

        ctx_loaded, wq_loaded, wk_loaded, wv_loaded = sem("ctx_loaded"), sem("wq_loaded"), sem("wk_loaded"), sem("wv_loaded")
        wo_loaded, wf_loaded, small_loaded, bias_loaded = sem("wo_loaded"), sem("wf_loaded"), sem("small_loaded"), sem("bias_loaded")
        ident_zero, ident_ready, diag_zeroed = sem("ident_zero"), sem("ident_ready"), sem("diag_zeroed")
        ctxT_done, ctxT_copied = sem("ctxT_done"), sem("ctxT_copied")
        k_done, k_copied, v_done, v_copied = sem("k_done"), sem("k_copied"), sem("v_done"), sem("v_copied")
        amax_ready, amax_shared, pow2_ready, scale_ready = sem("amax_ready"), sem("amax_shared"), sem("pow2_ready"), sem("scale_ready")
        wqT_done, wqT_hi, wqT_lo = sem("wqT_done"), sem("wqT_hi"), sem("wqT_lo")
        k_hi, k_lo, v_hi, v_lo = sem("k_hi"), sem("k_lo"), sem("v_hi"), sem("v_lo")
        wo_hi, wo_lo, wf_hi, wf_lo = sem("wo_hi"), sem("wo_lo"), sem("wf_hi"), sem("wf_lo")
        a_done, a_hi, a_lo = sem("a_done"), sem("a_hi"), sem("a_lo")
        vwT_done, vwT_even, vwT_odd = sem("vwT_done"), sem("vwT_even"), sem("vwT_odd")
        vw_done, vw_hi, vw_lo = sem("vw_done"), sem("vw_hi"), sem("vw_lo")
        pick_step, idx_ready, gate_ready, loop_scales, bias_ready = sem("pick_step"), sem("idx_ready"), sem("gate_ready"), sem("loop_scales"), sem("bias_ready")
        consts_set = sem("consts_set")
        x_loaded = [sem(f"x_loaded{r}") for r in range(4)]
        out_stored = [sem(f"out_stored{r}") for r in range(2)]
        x_stats, x_var, x_rstd, xn_ready, res_ready = sem("x_stats"), sem("x_var"), sem("x_rstd"), sem("xn_ready"), sem("res_ready")
        ve1_ready, ve2_ready = sem("ve1_ready"), sem("ve2_ready")
        xT_done, xT_hi, xT_lo = sem("xT_done"), sem("xT_hi"), sem("xT_lo")
        s_done, mx_ready, shifted, exp_done, sum_ready, rsum_ready, p_ready = (
            sem("s_done"), sem("mx_ready"), sem("shifted"), sem("exp_done"), sem("sum_ready"), sem("rsum_ready"), sem("p_ready"))
        pT_done, pT_hi, pT_lo = sem("pT_done"), sem("pT_hi"), sem("pT_lo")
        o_done, x2_ready, x2_stats, x2_var, x2_rstd, xn2_ready, x2b_ready = (
            sem("o_done"), sem("x2_ready"), sem("x2_stats"), sem("x2_var"), sem("x2_rstd"), sem("xn2_ready"), sem("x2b_ready"))
        x2T_done, x2T_hi, x2T_lo = sem("x2T_done"), sem("x2T_hi"), sem("x2T_lo")
        f_done, out_ready = sem("f_done"), sem("out_ready")

        block = stack.enter_context(nc.Block())

        def tile(q, b, lag):
            return q + (b + lag) // B, (b + lag) % B

        def valid(q):
            return not isinstance(q, int) or 0 <= q < NQ

        def nth(q, b):
            return q * B + b

        def positive(q, b, back):
            return not isinstance(q, int) or q * B + b - back >= 0

        def steps(eng, step):
            for n in range(-2, FIRST):
                step(*tile(0, 0, n))
            with eng.Fori(FIRST // B, FIRST // B + LOOPS) as q:
                for n in range(B):
                    step(*tile(q, FIRST % B, n))
            for n in range(FIRST + LOOPS * B, NT + 4):
                step(*tile(0, 0, n))

        @block.sync
        def _(sp):
            sp.dma_start(ctx_raw, ctx_in.rearrange("b j d -> j b d")).then_inc(ctx_loaded, 16)
            sp.dma_start(wk_raw, wk.rearrange("(k p) n -> p k n", p=P)).then_inc(wk_loaded, 16)
            sp.dma_start(wq_raw, wq.rearrange("(k p) n -> p k n", p=P)).then_inc(wq_loaded, 16)
            sp.dma_start(wv_raw, wv.rearrange("(k p) n -> p k n", p=P)).then_inc(wv_loaded, 16)
            sp.wait_ge(idx_ready, 1)
            op = sp.value_load(pick_idx[0:1, 0:1], min_val=0, max_val=NOPS - 1)
            sp.dma_start(wf_raw, ffn_w[bass.ds(op, 1), :, :].rearrange("o (k p) n -> p (o k) n", p=P)).then_inc(wf_loaded, 16)
            sp.wait_ge(wf_lo, 1)
            sp.wait_ge(wf_hi, 1)
            sp.dma_start(wo_raw, wo.rearrange("(h p) n -> p h n", p=P)).then_inc(wo_loaded, 16)
            sp.wait_ge(vw_lo, B * KT * NG)
            sp.dma_start(xin[:, 0, :], x[0, 0:P, :]).then_inc(x_loaded[0], 16)
            sp.dma_start(xin[:, 1, :], x[1, 0:P, :]).then_inc(x_loaded[1], 16)
            sp.dma_start(bias[:, 0, :], bo.rearrange("(a n) -> a n", a=1).to_broadcast([P, D])).then_inc(bias_loaded, 16)
            sp.dma_start(bias[:, 1, :], ffn_b[bass.ds(op, 1), :].to_broadcast([P, D])).then_inc(bias_loaded, 16)

            def step(q, b):
                qo, bo_ = tile(q, b, -3)
                if valid(qo):
                    sp.wait_ge(out_ready, nth(qo, bo_) + 1)
                    sp.dma_start(out[bo_, bass.ds(qo * P, P), :], outb[:, bo_ % 2, :]).then_inc(out_stored[bo_ % 2], 16)
                ql, bl = tile(q, b, 4)
                if valid(ql):
                    if positive(ql, bl, 4):
                        sp.wait_ge(xn_ready, nth(ql, bl) - 3)
                        sp.wait_ge(res_ready, nth(ql, bl) - 3)
                    sp.dma_start(xin[:, bl, :], x[bl, bass.ds(ql * P, P), :]).then_inc(x_loaded[bl], 16)

            steps(sp, step)
            for r in range(2):
                sp.wait_ge(out_stored[r], 16 * (NT // 2))

        @block.gpsimd
        def _(pool):
            nc.gpsimd.memset(ident[:, :], 0.0).then_inc(ident_zero, 1)
            pool.wait_ge(ident_zero, 1)
            nc.gpsimd.affine_select(out=ident[:, :], in_=ident[:, :], compare_op=ALU.not_equal, fill=1.0, base=0,
                                    pattern=[[-1, P]], channel_multiplier=1).then_inc(ident_ready, 1)
            nc.gpsimd.memset(neg_half, -0.5).then_inc(consts_set, 1)
            nc.gpsimd.memset(eps, EPS).then_inc(consts_set, 1)
            pool.wait_ge(consts_set, 2)
            nc.gpsimd.memset(diag[:, :, :, :, :].rearrange("p s h e n -> p (s h e n)").bitcast(U32), 0).then_inc(diag_zeroed, 1)
            for n, k in enumerate((WQ, KK, WF, VV, WO)):
                pool.wait_ge(amax_ready, n + 1)
                nc.gpsimd.partition_all_reduce(amax_all[:, k:k + 1], amax[:, k:k + 1], P,
                                               bass.bass_isa.ReduceOp.max).then_inc(amax_shared, 1)
            pool.wait_ge(vw_lo, B * KT * NG)

            def step(q, b):
                q2, b2 = tile(q, b, -2)
                q1, b1 = tile(q, b, 1)
                if valid(q2):
                    pool.wait_ge(x2_var, nth(q2, b2) + 1)
                    nc.gpsimd.tensor_tensor(ve2, mv2[:, 1:2], eps, ALU.add).then_inc(ve2_ready, 1)
                    pool.wait_ge(ve2_ready, nth(q2, b2) + 1)
                    nc.gpsimd.tensor_tensor(rstd2, ve2, neg_half, ALU.pow).then_inc(x2_rstd, 1)
                if valid(q1):
                    pool.wait_ge(x_var, nth(q1, b1) + 1)
                    nc.gpsimd.tensor_tensor(ve1, mv1[:, 1:2], eps, ALU.add).then_inc(ve1_ready, 1)
                    pool.wait_ge(ve1_ready, nth(q1, b1) + 1)
                    nc.gpsimd.tensor_tensor(rstd1, ve1, neg_half, ALU.pow).then_inc(x_rstd, 1)
                    if isinstance(q, int) and nth(q1, b1) == 0:
                        pool.wait_ge(bias_loaded, 32)
                        for k in range(2):
                            nc.gpsimd.tensor_scalar(bias[:, k, :], bias[:, k, :], gates[:, k:k + 1], None, ALU.mult).then_inc(bias_ready, 1)
                        pool.wait_ge(bias_ready, 2)
                    if positive(q1, b1, 4):
                        pool.wait_ge(out_ready, nth(q1, b1) - 3)
                    nc.gpsimd.tensor_tensor(res[:, b1, :], xin[:, b1, :], bias[:, 0, :], ALU.add).then_inc(res_ready, 1)
                if valid(q2):
                    pool.wait_ge(xn2_ready, nth(q2, b2) + 1)
                    nc.gpsimd.tensor_tensor(res[:, b2, :], res[:, b2, :], bias[:, 1, :], ALU.add).then_inc(x2b_ready, 1)

            steps(pool, step)

        @block.scalar
        def _(act):
            act.dma_start(pick[0:1, 0:NOPS], logits.rearrange("(a n) -> a n", a=1)).then_inc(small_loaded, 16)
            act.dma_start(pick[0:1, 8:8 + NOPS], u.rearrange("(a n) -> a n", a=1)).then_inc(small_loaded, 16)
            act.dma_start(gate_in[:, 0:1], g_xattn.rearrange("(a n) -> a n", a=1).to_broadcast([P, 1])).then_inc(small_loaded, 16)
            act.dma_start(gate_in[:, 1:2], g_ffn.rearrange("(a n) -> a n", a=1).to_broadcast([P, 1])).then_inc(small_loaded, 16)
            act.wait_ge(small_loaded, 64)
            nc.scalar.activation(gates, gate_in, ACT.Tanh).then_inc(gate_ready, 1)
            act.wait_ge(pick_step, 2)
            nc.scalar.activation(pick[0:1, 24:32], pick[0:1, 16:24], ACT.Exp, accum_out=pick[0:1, 32:33]).then_inc(pick_step, 1)
            act.wait_ge(pick_step, 3)
            nc.scalar.activation(pick[0:1, 33:34], pick[0:1, 32:33], ACT.Ln).then_inc(pick_step, 1)
            nc.scalar.activation(pick[0:1, 40:48], pick[0:1, 8:16], ACT.Ln).then_inc(pick_step, 1)
            act.wait_ge(pick_step, 5)
            nc.scalar.activation(pick[0:1, 48:56], pick[0:1, 40:48], ACT.Ln, scale=-1.0).then_inc(pick_step, 1)

            for b in range(B):
                act.wait_ge(ctxT_done, b + 1)
                nc.scalar.copy(ctxT[:, :, b * J:(b + 1) * J],
                               banks[:, b, 0:CT * J].rearrange("p (k n) -> p k n", k=CT)).then_inc(ctxT_copied, 1)
            for h in range(HP):
                act.wait_ge(k_done, h + 1)
                nc.scalar.copy(kvT[:, h, :], banks[:, h, 0:BJ]).then_inc(k_copied, 1)
            act.wait_ge(scale_ready, 1)
            for h in range(HP):
                act.wait_ge(wqT_done, h + 1)
                nc.scalar.activation(wqT[:, 0, h, :], banks[:, h, :], ACT.Copy, scale=scl[:, WQ:WQ + 1]).then_inc(wqT_hi, 1)

            def diagonal_hi(k, done):
                for e in range(2):
                    rows = slice(DH * e, DH * e + DH)
                    nc.scalar.activation(diag[rows, 0, :, e, :], kvT[rows, :, :], ACT.Copy,
                                         scale=scl[rows, k:k + 1]).then_inc(done, 1)

            act.wait_ge(scale_ready, 2)
            act.wait_ge(diag_zeroed, 1)
            diagonal_hi(KK, k_hi)
            act.wait_ge(scale_ready, 3)
            act.wait_ge(wf_loaded, 16)
            nc.scalar.activation(wf_split[:, 0, :, :], wf_raw, ACT.Copy, scale=scl[:, WF:WF + 1]).then_inc(wf_hi, 1)
            with act.Fori(0, HP) as h:
                for e in range(2):
                    for k in range(KT):
                        act.wait_ge(a_done, h * (2 * KT) + (e * KT + k + 1))
                        nc.scalar.activation(
                            a_split[:, 0, k, :, bass.ds(h * (2 * J) + e * J, J)],
                            banks[:, e * KT + k, 0:BJ].rearrange("p (b n) -> p b n", b=B),
                            ACT.Copy, scale=2.0 ** FOLD_BITS).then_inc(a_hi, 1)
            for h in range(HP):
                act.wait_ge(v_done, h + 1)
                if h == 0:
                    act.wait_ge(k_lo, 2)
                nc.scalar.copy(kvT[:, h, :], banks[:, h, 0:BJ]).then_inc(v_copied, 1)
            act.wait_ge(scale_ready, 4)
            act.wait_ge(a_done, HEADS * KT)
            diagonal_hi(VV, v_hi)
            act.wait_ge(scale_ready, 5)
            act.wait_ge(ctxT_done, B)
            nc.scalar.activation(wo_split[:, 0, :, :], wo_raw, ACT.Copy, scale=scl[:, WO:WO + 1]).then_inc(wo_hi, 1)
            act.wait_ge(wo_lo, 1)
            with act.Fori(0, KT) as t:
                for h in range(0, HEADS, 2):
                    act.wait_ge(vwT_done, t * HEADS + (h + 1))
                    nc.scalar.copy(vwT[:, :, h * J:(h + 1) * J],
                                   banks[:, h % 8, 0:BJ].rearrange("p (b n) -> p b n", b=B)).then_inc(vwT_even, 1)
                for n in range(B * NG):
                    b, g = n // NG, n % NG
                    cs = GROUPS[g]
                    act.wait_ge(vw_done, t * (B * NG) + (n + 1))
                    nc.scalar.activation(vw[:, b, 0, cs.start:cs.stop, bass.ds(t * P, P)],
                                         banks[:, n % 8, 0:len(cs) * P].rearrange("p (c n) -> p c n", n=P),
                                         ACT.Copy, scale=2.0 ** FOLD_BITS).then_inc(vw_hi, 1)

            act.wait_ge(loop_scales, 3)

            def step(q, b):
                q1, b1 = tile(q, b, -1)
                q2, b2 = tile(q, b, -2)
                q3, b3 = tile(q, b, 1)

                def probs_hi(g):
                    cs = GROUPS[g]
                    act.wait_ge(pT_done, nth(q1, b1) * NG + (g + 1))
                    nc.scalar.activation(pT[:, 0, cs.start:cs.stop, :],
                                         pt_ps[g % 2][:, 0:len(cs) * P].rearrange("p (c n) -> p c n", n=P),
                                         ACT.Copy, scale=2.0 ** PROB_BITS).then_inc(pT_hi, 1)

                if valid(q1):
                    if positive(q1, b1, 1):
                        act.wait_ge(o_done, nth(q1, b1))
                    probs_hi(0)
                    probs_hi(1)
                if valid(q2):
                    act.wait_ge(x2T_done, nth(q2, b2) + 1)
                    if positive(q2, b2, 1):
                        act.wait_ge(f_done, nth(q2, b2))
                    nc.scalar.activation(x2T[:, 0, :, :], t_ps[:, :].rearrange("p (k n) -> p k n", n=P), ACT.Copy,
                                         scale=2.0 ** XN_BITS).then_inc(x2T_hi, 1)
                if valid(q1):
                    probs_hi(2)
                if valid(q):
                    act.wait_ge(shifted, nth(q, b) + 1)
                    nc.scalar.activation(probs[:, b % 2, :], probs[:, b % 2, :], ACT.Exp,
                                         scale=exp_scale).then_inc(exp_done, 1)
                if valid(q3):
                    act.wait_ge(xT_done, nth(q3, b3) + 1)
                    if positive(q3, b3, 1):
                        act.wait_ge(s_done, nth(q3, b3))
                    nc.scalar.activation(xT[:, 0, :, :], t_ps[:, :].rearrange("p (k n) -> p k n", n=P), ACT.Copy,
                                         scale=2.0 ** XN_BITS).then_inc(xT_hi, 1)

            steps(act, step)

        @block.vector
        def _(dve):
            lg, uu, sh = pick[0:1, 0:8], pick[0:1, 8:16], pick[0:1, 16:24]
            dve.wait_ge(small_loaded, 64)
            nc.vector.reduce_max(pick[0:1, 34:35], lg, AX.X).then_inc(pick_step, 1)
            dve.wait_ge(pick_step, 1)
            nc.vector.tensor_scalar(sh, lg, pick[0:1, 34:35], None, ALU.subtract).then_inc(pick_step, 1)
            dve.wait_ge(pick_step, 6)
            nc.vector.tensor_scalar(pick[0:1, 56:64], sh, pick[0:1, 33:34], None, ALU.subtract).then_inc(pick_step, 1)
            dve.wait_ge(pick_step, 7)
            nc.vector.tensor_tensor(pick[0:1, 64:72], pick[0:1, 56:64], pick[0:1, 48:56], ALU.subtract).then_inc(pick_step, 1)
            dve.wait_ge(pick_step, 8)
            nc.vector.max(pick[0:1, 72:80], pick[0:1, 64:72]).then_inc(pick_step, 1)
            dve.wait_ge(pick_step, 9)
            nc.vector.max_index(pick_idx[0:1, :], pick[0:1, 72:80], pick[0:1, 64:72]).then_inc(idx_ready, 1)

            count = [0]

            def power_of_two_scale(k, data, axis, bits):
                n = count[0] = count[0] + 1
                nc.vector.tensor_reduce(amax[:, k:k + 1], data, axis, ALU.max, apply_absolute_value=True).then_inc(amax_ready, 1)
                dve.wait_ge(amax_shared, n)
                nc.vector.tensor_scalar(amax[:, k:k + 1], amax_all[:, k:k + 1], 1e-30, None, ALU.max).then_inc(pow2_ready, 1)
                dve.wait_ge(pow2_ready, 3 * n - 2)
                nc.vector.tensor_scalar(pow2[:, k:k + 1].bitcast(U32), amax[:, k:k + 1].bitcast(U32), 0x7F800000, None,
                                        ALU.bitwise_and).then_inc(pow2_ready, 1)
                dve.wait_ge(pow2_ready, 3 * n - 1)
                nc.vector.tensor_scalar(pow2[:, k:k + 1], pow2[:, k:k + 1], 2.0 ** -bits, None, ALU.mult).then_inc(pow2_ready, 1)
                dve.wait_ge(pow2_ready, 3 * n)
                nc.vector.reciprocal(scl[:, k:k + 1], pow2[:, k:k + 1]).then_inc(scale_ready, 1)
                dve.wait_ge(scale_ready, n)

            def low(lo, value, scale, hi):
                return nc.vector.scalar_tensor_tensor(out=lo, in0=value, scalar=scale, in1=hi, op0=ALU.mult, op1=ALU.subtract)

            def diagonal_lo(k, hi_ready, done):
                for e in range(2):
                    rows = slice(DH * e, DH * e + DH)
                    dve.wait_ge(hi_ready, e + 1)
                    low(diag[rows, 1, :, e, :], kvT[rows, :, :], scl[rows, k:k + 1], diag[rows, 0, :, e, :]).then_inc(done, 1)

            dve.wait_ge(wq_loaded, 16)
            power_of_two_scale(WQ, wq_raw, AX.XY, OPERAND_BITS)
            dve.wait_ge(k_copied, HP)
            power_of_two_scale(KK, kvT, AX.XY, OPERAND_BITS)
            for h in range(HP):
                dve.wait_ge(wqT_hi, h + 1)
                low(wqT[:, 1, h, :], banks[:, h, :], scl[:, WQ:WQ + 1], wqT[:, 0, h, :]).then_inc(wqT_lo, 1)
            diagonal_lo(KK, k_hi, k_lo)
            dve.wait_ge(wf_loaded, 16)
            power_of_two_scale(WF, wf_raw, AX.XY, WF_BITS)
            dve.wait_ge(wf_hi, 1)
            low(wf_split[:, 1, :, :].rearrange("p k n -> p (k n)"), wf_raw.rearrange("p k n -> p (k n)"), scl[:, WF:WF + 1],
                wf_split[:, 0, :, :].rearrange("p k n -> p (k n)")).then_inc(wf_lo, 1)
            with dve.Fori(0, HP) as h:
                for e in range(2):
                    for k in range(KT):
                        dve.wait_ge(a_hi, h * (2 * KT) + (e * KT + k + 1))
                        low(a_split[:, 1, k, :, bass.ds(h * (2 * J) + e * J, J)],
                            banks[:, e * KT + k, 0:BJ].rearrange("p (b n) -> p b n", b=B), 2.0 ** FOLD_BITS,
                            a_split[:, 0, k, :, bass.ds(h * (2 * J) + e * J, J)]).then_inc(a_lo, 1)
            dve.wait_ge(v_copied, HP)
            power_of_two_scale(VV, kvT, AX.XY, OPERAND_BITS)
            diagonal_lo(VV, v_hi, v_lo)
            dve.wait_ge(wo_loaded, 16)
            power_of_two_scale(WO, wo_raw, AX.XY, OPERAND_BITS)
            dve.wait_ge(wo_hi, 1)
            low(wo_split[:, 1, :, :].rearrange("p k n -> p (k n)"), wo_raw.rearrange("p k n -> p (k n)"), scl[:, WO:WO + 1],
                wo_split[:, 0, :, :].rearrange("p k n -> p (k n)")).then_inc(wo_lo, 1)

            back = [2.0 ** (-FOLD_BITS - XN_BITS) * DH ** -0.5, 2.0 ** (-FOLD_BITS - PROB_BITS), 2.0 ** -XN_BITS]
            dve.wait_ge(gate_ready, 1)
            nc.vector.scalar_tensor_tensor(out=exp_scale, in0=pow2[:, KK:KK + 1], scalar=back[0], in1=pow2[:, WQ:WQ + 1],
                                           op0=ALU.mult, op1=ALU.mult).then_inc(loop_scales, 1)
            nc.vector.scalar_tensor_tensor(out=amax[:, 7:8], in0=pow2[:, VV:VV + 1], scalar=back[1], in1=pow2[:, WO:WO + 1],
                                           op0=ALU.mult, op1=ALU.mult).then_inc(loop_scales, 1)
            nc.vector.scalar_tensor_tensor(out=f_scale, in0=pow2[:, WF:WF + 1], scalar=back[2], in1=gates[:, 1:2],
                                           op0=ALU.mult, op1=ALU.mult).then_inc(loop_scales, 1)
            dve.wait_ge(loop_scales, 3)
            nc.vector.tensor_tensor(o_scale, amax[:, 7:8], gates[:, 0:1], ALU.mult).then_inc(loop_scales, 1)

            with dve.Fori(0, KT) as t:
                for h in range(1, HEADS, 2):
                    dve.wait_ge(vwT_done, t * HEADS + (h + 1))
                    nc.vector.tensor_copy(vwT[:, :, h * J:(h + 1) * J],
                                          banks[:, h % 8, 0:BJ].rearrange("p (b n) -> p b n", b=B)).then_inc(vwT_odd, 1)
                for n in range(B * NG):
                    b, g = n // NG, n % NG
                    cs = GROUPS[g]
                    dve.wait_ge(vw_hi, t * (B * NG) + (n + 1))
                    low(vw[:, b, 1, cs.start:cs.stop, bass.ds(t * P, P)],
                        banks[:, n % 8, 0:len(cs) * P].rearrange("p (c n) -> p c n", n=P), 2.0 ** FOLD_BITS,
                        vw[:, b, 0, cs.start:cs.stop, bass.ds(t * P, P)]).then_inc(vw_lo, 1)

            dve.wait_ge(loop_scales, 4)
            dve.wait_ge(vw_lo, B * KT * NG)

            FH = FULL * HB

            def by_head(ap):
                return ap.rearrange("p (h n) -> p h n", n=J)

            def step(q, b):
                qp, bp = tile(q, b, -1)
                q2, b2 = tile(q, b, -2)
                q3, b3 = tile(q, b, -3)
                qn, bn = tile(q, b, 1)

                def probs_lo(g):
                    cs = GROUPS[g]
                    dve.wait_ge(pT_hi, nth(qp, bp) * NG + (g + 1))
                    low(pT[:, 1, cs.start:cs.stop, :].rearrange("p c n -> p (c n)"), pt_ps[g % 2][:, 0:len(cs) * P],
                        2.0 ** PROB_BITS, pT[:, 0, cs.start:cs.stop, :].rearrange("p c n -> p (c n)")).then_inc(pT_lo, 1)

                if valid(q2):
                    dve.wait_ge(o_done, nth(q2, b2) + 1)
                    dve.wait_ge(res_ready, nth(q2, b2) + 1)
                    nc.vector.scalar_tensor_tensor(out=res[:, b2, :], in0=o_ps, scalar=o_scale, in1=res[:, b2, :],
                                                   op0=ALU.mult, op1=ALU.add).then_inc(x2_ready, 1)
                    dve.wait_ge(x2_ready, nth(q2, b2) + 1)
                    nc.vector.bn_stats(bn2, res[:, b2, :]).then_inc(x2_stats, 1)
                    dve.wait_ge(x2_stats, nth(q2, b2) + 1)
                if valid(qn):
                    dve.wait_ge(x_loaded[bn], qn * 16 + 16)
                    nc.vector.bn_stats(bn1, xin[:, bn, :]).then_inc(x_stats, 1)
                if valid(q2):
                    nc.vector.bn_aggr(mv2, bn2).then_inc(x2_var, 1)
                if valid(qn):
                    dve.wait_ge(x_stats, nth(qn, bn) + 1)
                if valid(qp):
                    probs_lo(0)
                if valid(qn):
                    nc.vector.bn_aggr(mv1, bn1).then_inc(x_var, 1)
                if valid(q2):
                    dve.wait_ge(x2_rstd, nth(q2, b2) + 1)
                    nc.vector.tensor_scalar(xn2, res[:, b2, :], mv2[:, 0:1], rstd2, ALU.subtract, ALU.mult).then_inc(xn2_ready, 1)
                if valid(qp):
                    probs_lo(1)
                if valid(qn):
                    dve.wait_ge(x_rstd, nth(qn, bn) + 1)
                    if positive(qn, bn, 1):
                        dve.wait_ge(xT_done, nth(qn, bn))
                    nc.vector.tensor_scalar(xn, xin[:, bn, :], mv1[:, 0:1], rstd1, ALU.subtract, ALU.mult).then_inc(xn_ready, 1)
                if valid(q3):
                    dve.wait_ge(f_done, nth(q3, b3) + 1)
                    dve.wait_ge(x2b_ready, nth(q3, b3) + 1)
                    if positive(q3, b3, 2):
                        dve.wait_ge(out_stored[b3 % 2], (q3 * 2 + b3 // 2) * 16)
                    nc.vector.scalar_tensor_tensor(out=outb[:, b3 % 2, :], in0=f_ps, scalar=f_scale, in1=res[:, b3, :],
                                                   op0=ALU.mult, op1=ALU.add).then_inc(out_ready, 1)
                if valid(q):
                    dve.wait_ge(s_done, nth(q, b) + 1)
                    nc.vector.reduce_max(mx[:, 0:FH].rearrange("p (k h) -> p k h", h=HB),
                                         s_ps[:, 0:FULL, 0:HB * J].rearrange("p k (h n) -> p k h n", n=J), AX.X).then_inc(mx_ready, 1)
                    nc.vector.reduce_max(mx[:, FH:HEADS], by_head(s_ps[:, FULL, 0:(HEADS - FH) * J]), AX.X).then_inc(mx_ready, 1)
                if valid(q2):
                    dve.wait_ge(x2T_hi, nth(q2, b2) + 1)
                    low(x2T[:, 1, :, :].rearrange("p k n -> p (k n)"), t_ps, 2.0 ** XN_BITS,
                        x2T[:, 0, :, :].rearrange("p k n -> p (k n)")).then_inc(x2T_lo, 1)
                if valid(q):
                    dve.wait_ge(mx_ready, nth(q, b) * 2 + 2)
                    if positive(q, b, 2):
                        dve.wait_ge(pT_done, (nth(q, b) - 1) * NG)
                    nc.vector.tensor_tensor(probs[:, b % 2, 0:FH * J].rearrange("p (k h n) -> p k h n", h=HB, n=J),
                                            s_ps[:, 0:FULL, 0:HB * J].rearrange("p k (h n) -> p k h n", n=J),
                                            mx[:, 0:FH].rearrange("p (k h) -> p k h", h=HB).unsqueeze(3).to_broadcast([P, FULL, HB, J]),
                                            ALU.subtract)
                    nc.vector.tensor_tensor(by_head(probs[:, b % 2, FH * J:HJ]), by_head(s_ps[:, FULL, 0:(HEADS - FH) * J]),
                                            mx[:, FH:HEADS].unsqueeze(2).to_broadcast([P, HEADS - FH, J]),
                                            ALU.subtract).then_inc(shifted, 1)
                if valid(qp):
                    probs_lo(2)
                if valid(qn):
                    dve.wait_ge(xT_hi, nth(qn, bn) + 1)
                    low(xT[:, 1, :, :].rearrange("p k n -> p (k n)"), t_ps, 2.0 ** XN_BITS,
                        xT[:, 0, :, :].rearrange("p k n -> p (k n)")).then_inc(xT_lo, 1)
                if valid(q):
                    dve.wait_ge(exp_done, nth(q, b) + 1)
                    nc.vector.reduce_sum(sums, by_head(probs[:, b % 2, :]), AX.X).then_inc(sum_ready, 1)
                    dve.wait_ge(sum_ready, nth(q, b) + 1)
                    nc.vector.reciprocal(rsum, sums).then_inc(rsum_ready, 1)
                    dve.wait_ge(rsum_ready, nth(q, b) + 1)
                    nc.vector.tensor_tensor(by_head(probs[:, b % 2, :]), by_head(probs[:, b % 2, :]),
                                            rsum.unsqueeze(2).to_broadcast([P, HEADS, J]), ALU.mult).then_inc(p_ready, 1)

            steps(dve, step)

        @block.tensor
        def _(pe):
            def split_products(ps, lhs, rhs, first, last):
                for n, (l, r) in enumerate(((0, 0), (0, 1), (1, 0))):
                    mm = nc.tensor.matmul(ps, lhs(l), rhs(r), start=first and n == 0, stop=last and n == 2)
                return mm

            pe.wait_ge(ident_ready, 1)
            pe.wait_ge(ctx_loaded, 16)
            for b in range(B):
                for k in range(CT):
                    mm = nc.tensor.transpose(banks[:, b, k * J:(k + 1) * J], ctx_raw[:, b, k * P:(k + 1) * P], ident[0:J, 0:J])
                mm.then_inc(ctxT_done, 1)
            pe.wait_ge(wk_loaded, 16)
            pe.wait_ge(ctxT_copied, B)
            for h in range(HP):
                for k in range(CT):
                    mm = nc.tensor.matmul(banks[:, h, 0:BJ], wk_raw[:, k, h * P:(h + 1) * P], ctxT[:, k, :],
                                          start=k == 0, stop=k == CT - 1)
                mm.then_inc(k_done, 1)
            pe.wait_ge(wq_loaded, 16)
            for h in range(HP):
                pe.wait_ge(k_copied, h + 1)
                for k in range(KT):
                    mm = nc.tensor.transpose(banks[:, h, k * P:(k + 1) * P], wq_raw[:, k, h * P:(h + 1) * P], ident[:, :])
                mm.then_inc(wqT_done, 1)
            pe.wait_ge(wqT_lo, HP)
            pe.wait_ge(k_lo, 2)

            def fold_k(h):
                for e in range(2):
                    for k in range(KT):
                        if not isinstance(h, int):
                            pe.wait_ge(a_lo, h * (2 * KT) + (e * KT + k + 1 - 2 * KT))
                        split_products(banks[:, e * KT + k, 0:BJ],
                                       lambda s: wqT[:, s, bass.ds(h, 1), k * P:(k + 1) * P].rearrange("p o n -> p (o n)"),
                                       lambda s: diag[:, s, bass.ds(h, 1), e, :].rearrange("p o n -> p (o n)"),
                                       True, True).then_inc(a_done, 1)

            fold_k(0)
            with pe.Fori(1, HP) as h:
                fold_k(h)
            pe.wait_ge(wv_loaded, 16)
            pe.wait_ge(a_lo, HEADS * KT)
            for h in range(HP):
                for k in range(CT):
                    mm = nc.tensor.matmul(banks[:, h, 0:BJ], wv_raw[:, k, h * P:(h + 1) * P], ctxT[:, k, :],
                                          start=k == 0, stop=k == CT - 1)
                mm.then_inc(v_done, 1)
            pe.wait_ge(v_copied, HP)
            pe.wait_ge(v_lo, 2)
            pe.wait_ge(wo_lo, 1)
            with pe.Fori(0, KT) as t:
                for h in range(HEADS):
                    if h < 8:
                        pass
                    elif h % 2 == 0:
                        pe.wait_ge(vwT_even, t * HP + (h - 8) // 2 + 1)
                    else:
                        pe.wait_ge(vwT_odd, t * HP + (h - 8) // 2 + 1)
                    split_products(banks[:, h % 8, 0:BJ],
                                   lambda s: wo_split[:, s, h // 2, bass.ds(t * P, P)],
                                   lambda s: diag[:, s, h // 2, h % 2, :], True, True).then_inc(vwT_done, 1)
                pe.wait_ge(vwT_even, t * HP + HP)
                pe.wait_ge(vwT_odd, t * HP + HP)
                for n in range(B * NG):
                    b, g = n // NG, n % NG
                    if n >= 8:
                        pe.wait_ge(vw_lo, t * (B * NG) + (n - 7))
                    for m, ch in enumerate(GROUPS[g]):
                        lo, hi = CHUNKS[ch]
                        mm = nc.tensor.transpose(banks[0:hi - lo, n % 8, m * P:(m + 1) * P], vwT[:, b, lo:hi], ident[:, :])
                    mm.then_inc(vw_done, 1)
                pe.wait_ge(vw_lo, t * (B * NG) + B * NG)
            pe.wait_ge(wf_lo, 1)

            def step(q, b):
                qp, bp = tile(q, b, -1)
                q2, b2 = tile(q, b, -2)
                qn, bn = tile(q, b, 1)

                def scores(ks):
                    for k in ks:
                        for l, r in ((0, 0), (0, 1), (1, 0)):
                            for n, (h0, h1) in enumerate(BANKS):
                                mm = nc.tensor.matmul(s_ps[:, n, 0:(h1 - h0) * J], xT[:, l, k, :], a_split[:, r, k, b, h0 * J:h1 * J],
                                                      start=k == 0 and l + r == 0, stop=k == KT - 1 and l == 1)
                    return mm

                def turn_probs(g):
                    for m, ch in enumerate(GROUPS[g]):
                        lo, hi = CHUNKS[ch]
                        mm = nc.tensor.transpose(pt_ps[g % 2][0:hi - lo, m * P:(m + 1) * P], probs[:, bp % 2, lo:hi], ident[:, :])
                    mm.then_inc(pT_done, 1)

                def attend(g):
                    pe.wait_ge(pT_lo, nth(qp, bp) * NG + (g + 1))
                    for ch in GROUPS[g]:
                        n = CHUNKS[ch][1] - CHUNKS[ch][0]
                        mm = split_products(o_ps, lambda s: pT[0:n, s, ch, :], lambda s: vw[0:n, bp, s, ch, :],
                                            ch == 0, ch == NC - 1)
                    return mm

                if valid(q):
                    pe.wait_ge(xT_lo, nth(q, b) + 1)
                    if positive(q, b, 1):
                        pe.wait_ge(shifted, nth(q, b))
                    scores(range(0, KT // 2))
                if valid(qp):
                    pe.wait_ge(p_ready, nth(qp, bp) + 1)
                    if positive(qp, bp, 1):
                        pe.wait_ge(pT_lo, nth(qp, bp) * NG)
                    turn_probs(0)
                    turn_probs(1)
                if valid(q):
                    scores(range(KT // 2, KT)).then_inc(s_done, 1)
                if valid(q2):
                    pe.wait_ge(xn2_ready, nth(q2, b2) + 1)
                    if valid(q):
                        pe.wait_ge(xT_lo, nth(q, b) + 1)
                    else:
                        pe.wait_ge(x2T_lo, nth(q2, b2))
                    for k in range(KT):
                        mm = nc.tensor.transpose(t_ps[:, k * P:(k + 1) * P], xn2[:, k * P:(k + 1) * P], ident[:, :])
                    mm.then_inc(x2T_done, 1)
                if valid(qp):
                    if positive(qp, bp, 1):
                        pe.wait_ge(x2_ready, nth(qp, bp))
                    attend(0)
                    turn_probs(2)
                if valid(qn):
                    pe.wait_ge(xn_ready, nth(qn, bn) + 1)
                    if valid(q2):
                        pe.wait_ge(x2T_lo, nth(q2, b2) + 1)
                    elif positive(qn, bn, 1):
                        pe.wait_ge(xT_lo, nth(qn, bn))
                    for k in range(KT):
                        mm = nc.tensor.transpose(t_ps[:, k * P:(k + 1) * P], xn[:, k * P:(k + 1) * P], ident[:, :])
                    mm.then_inc(xT_done, 1)
                if valid(qp):
                    attend(1)
                if valid(q2):
                    pe.wait_ge(x2T_lo, nth(q2, b2) + 1)
                    if positive(q2, b2, 1):
                        pe.wait_ge(out_ready, nth(q2, b2))
                    for k in range(KT):
                        mm = split_products(f_ps, lambda s: x2T[:, s, k, :], lambda s: wf_split[:, s, k, :], k == 0, k == KT - 1)
                    mm.then_inc(f_done, 1)
                if valid(qp):
                    attend(2).then_inc(o_done, 1)

            steps(pe, step)


_INS = ["x", "ctx_768", "g_xattn", "g_ffn", "L0_xattn_Wq", "L0_xattn_Wk", "L0_xattn_Wv", "L0_xattn_Wo", "L0_xattn_bo",
        "L0_ffn_W", "L0_ffn_b", "L0_ffn_logits", "L0_ffn_u"]


def kernel(**inputs):
    import numpy as np
    import concourse.bacc as bacc
    from concourse import mybir as mb
    from concourse.bass_utils import run_bass_kernel_spmd

    nc = bacc.Bacc("TRN2", target_bir_lowering=False, num_devices=1, dynamic_dma_scratch_size=1024)
    arrays, args = {}, []
    for name in _INS:
        a = np.ascontiguousarray(inputs[name])
        arrays[f"in_{name}"] = a
        args.append(nc.dram_tensor(f"in_{name}", a.shape, mb.dt.from_np(a.dtype), kind="ExternalInput").ap())
    shape = inputs["x"].shape
    args.append(nc.dram_tensor("out_0", shape, mb.dt.float32, kind="ExternalOutput").ap())
    flamingo_layer(nc, *args)
    r = run_bass_kernel_spmd(nc, [arrays], core_ids=[0])
    return r.results[0]["out_0"]
```

```python
from contextlib import ExitStack

import concourse.bass as bass
from concourse import mybir

ALU = mybir.AluOpType
ACT = mybir.ActivationFunctionType
AX = mybir.AxisListType
F32 = mybir.dt.float32
F16 = mybir.dt.float16
U32 = mybir.dt.uint32

P = 128
HEADS = 16
DH = 64
EPS = 1e-5
OPERAND_BITS = 10
FOLD_BITS = -13
XN_BITS = 8
PROB_BITS = 14
WF_BITS = 13


def flamingo_layer(nc, x, ctx_in, g_xattn, g_ffn, wq, wk, wv, wo, bo, ffn_w, ffn_b, logits, u, out):
    B, SQ, D = x.shape
    _, J, CD = ctx_in.shape
    ID = HEADS * DH
    HJ = HEADS * J
    NOPS = ffn_w.shape[0]
    KT = D // P
    CT = CD // P
    HP = ID // P
    BJ = B * J
    NQ = SQ // P
    CHUNKS = [(c, min(c + P, HJ)) for c in range(0, HJ, P)]
    NC = len(CHUNKS)
    GROUPS = [range(0, 4), range(4, 8), range(8, NC)]
    NG = len(GROUPS)
    HB = 512 // J
    BANKS = [(h, min(h + HB, HEADS)) for h in range(0, HEADS, HB)]
    NT = B * NQ
    FIRST = 6
    LOOPS = (NT - 3 - FIRST) // B
    assert B == 4 and D == 512 and len(BANKS) == 3
    FULL = len(BANKS) - 1

    with ExitStack() as stack:
        def sb(name, shape, dt=F32):
            return stack.enter_context(nc.sbuf_tensor(name, shape, dt))

        def sem(name):
            return stack.enter_context(nc.semaphore(name))

        a_split = sb("a_split", [P, 2, KT, B, HJ], F16)
        wf_split = sb("wf_split", [P, 2, KT, D], F16)
        VW_WORDS = B * 2 * NC * D // 2
        vw_arena = sb("vw_arena", [P, VW_WORDS])
        vw = vw_arena[:, :].bitcast(F16).rearrange("p (b s c d) -> p b s c d", b=B, s=2, c=NC)
        LOOP_WORDS = HP * D + B * HJ + 2 * HP * BJ
        arena = sb("arena", [P, LOOP_WORDS])
        ident = sb("ident", [P, P])
        cst = sb("cst", [P, 64])
        stats = sb("stats", [P, 64])
        pick = sb("pick", [1, 80])
        pick_idx = sb("pick_idx", [1, 8], U32)

        class Carve:
            def __init__(self, base):
                self.base, self.at = base, 0

            def take(self, words):
                self.at += words
                return self.base[:, self.at - words:self.at]

        c = Carve(vw_arena)
        wq_raw = c.take(KT * ID).rearrange("p (k n) -> p k n", k=KT)
        wk_raw = c.take(CT * ID).rearrange("p (k n) -> p k n", k=CT)
        wv_raw = c.take(CT * ID).rearrange("p (k n) -> p k n", k=CT)
        wqT = c.take(HP * D).bitcast(F16).rearrange("p (s h n) -> p s h n", s=2, h=HP)
        ctxT = c.take(CT * BJ).rearrange("p (k n) -> p k n", k=CT)
        kvT = c.take(HP * BJ).rearrange("p (h n) -> p h n", h=HP)
        assert c.at <= VW_WORDS, c.at
        c = Carve(arena)
        wo_split = c.take(HP * D).bitcast(F16).rearrange("p (s h n) -> p s h n", s=2, h=HP)
        vwT_words = B * HJ
        at_vwT = c.at
        vwT = c.take(vwT_words).rearrange("p (b n) -> p b n", b=B)
        wo_raw = arena[:, at_vwT:at_vwT + HP * D].rearrange("p (h n) -> p h n", h=HP)
        diag = c.take(2 * HP * 2 * BJ // 2).bitcast(F16).rearrange("p (s h e n) -> p s h e n", s=2, h=HP, e=2)
        assert c.at <= LOOP_WORDS, c.at
        ctx_raw = arena[0:J, 0:B * CD].rearrange("p (b n) -> p b n", b=B)
        wf_raw = arena[:, at_vwT:at_vwT + KT * D].rearrange("p (k n) -> p k n", k=KT)

        c = Carve(arena)
        xin = c.take(2 * D).rearrange("p (r n) -> p r n", r=2)
        res = c.take(4 * D).rearrange("p (r n) -> p r n", r=4)
        outb = c.take(2 * D).rearrange("p (r n) -> p r n", r=2)
        xn, x2n = c.take(D), c.take(D)
        xs = c.take(D).bitcast(F16).rearrange("p (s n) -> p s n", s=2)
        x2s = c.take(D).bitcast(F16).rearrange("p (s n) -> p s n", s=2)
        xT = c.take(D).bitcast(F16).rearrange("p (s k n) -> p s k n", s=2, k=KT)
        x2T = c.take(D).bitcast(F16).rearrange("p (s k n) -> p s k n", s=2, k=KT)
        probs = c.take(HJ)
        ps = c.take(NC * P).bitcast(F16).rearrange("p (s n) -> p s n", s=2)
        pT = c.take(NC * P).bitcast(F16).rearrange("p (s c n) -> p s c n", s=2, c=NC)
        bias = c.take(2 * D).rearrange("p (k n) -> p k n", k=2)
        assert c.at <= LOOP_WORDS, c.at

        amax, pow2, scl = cst[:, 0:8], cst[:, 8:16], cst[:, 16:24]
        WQ, KK, VV, WO, WF = range(5)
        amax_all = cst[:, 24:32]
        exp_scale, o_scale, f_scale = cst[:, 32:33], cst[:, 33:34], cst[:, 34:35]
        gates, gate_in = cst[:, 36:38], cst[:, 38:40]
        neg_half = cst[:, 40:41]
        eps = cst[:, 41:42]
        bn1, mv1, rstd1, ve1 = stats[:, 0:6], stats[:, 6:8], stats[:, 8:9], stats[:, 9:10]
        bn2, mv2, rstd2, ve2 = stats[:, 12:18], stats[:, 18:20], stats[:, 20:21], stats[:, 21:22]
        mx, sums, rsum = stats[:, 24:40], stats[:, 40:56], cst[:, 44:60]

        banks = stack.enter_context(nc.psum_tensor("banks", [P, 8, 512], F32))
        s_ps = banks[:, 0:3, :]
        o_ps, f_ps = banks[:, 3, :], banks[:, 4, :]

        ctx_loaded, wq_loaded, wk_loaded, wv_loaded = sem("ctx_loaded"), sem("wq_loaded"), sem("wk_loaded"), sem("wv_loaded")
        wo_loaded, wf_loaded, small_loaded, bias_loaded = sem("wo_loaded"), sem("wf_loaded"), sem("small_loaded"), sem("bias_loaded")
        ident_zero, ident_ready, diag_zeroed = sem("ident_zero"), sem("ident_ready"), sem("diag_zeroed")
        ctxT_done, ctxT_copied = sem("ctxT_done"), sem("ctxT_copied")
        k_done, k_copied, v_done, v_copied = sem("k_done"), sem("k_copied"), sem("v_done"), sem("v_copied")
        amax_ready, amax_shared, pow2_ready, scale_ready = sem("amax_ready"), sem("amax_shared"), sem("pow2_ready"), sem("scale_ready")
        wqT_done, wqT_hi, wqT_lo = sem("wqT_done"), sem("wqT_hi"), sem("wqT_lo")
        k_hi, k_lo, v_hi, v_lo = sem("k_hi"), sem("k_lo"), sem("v_hi"), sem("v_lo")
        wo_hi, wo_lo, wf_hi, wf_lo = sem("wo_hi"), sem("wo_lo"), sem("wf_hi"), sem("wf_lo")
        a_done, a_hi, a_lo = sem("a_done"), sem("a_hi"), sem("a_lo")
        vwT_done, vwT_even, vwT_odd = sem("vwT_done"), sem("vwT_even"), sem("vwT_odd")
        vw_done, vw_hi, vw_lo = sem("vw_done"), sem("vw_hi"), sem("vw_lo")
        pick_step, idx_ready, gate_ready, loop_scales, bias_ready = sem("pick_step"), sem("idx_ready"), sem("gate_ready"), sem("loop_scales"), sem("bias_ready")
        consts_set = sem("consts_set")
        x_loaded = [sem(f"x_loaded{r}") for r in range(2)]
        turn_due = sem("turn_due")
        out_stored = [sem(f"out_stored{r}") for r in range(2)]
        x_stats, x_var, ve1_ready, x_rstd, xn_ready, res_ready = (
            sem("x_stats"), sem("x_var"), sem("ve1_ready"), sem("x_rstd"), sem("xn_ready"), sem("res_ready"))
        x_hi, x_lo, xT_turned = sem("x_hi"), sem("x_lo"), sem("xT_turned")
        s_done, mx_ready, shifted, exp_done = sem("s_done"), sem("mx_ready"), sem("shifted"), sem("exp_done")
        sum_ready, rsum_ready, p_ready, p_hi, p_lo, pT_turned, pad_zeroed = (
            sem("sum_ready"), sem("rsum_ready"), sem("p_ready"), sem("p_hi"), sem("p_lo"), sem("pT_turned"), sem("pad_zeroed"))
        o_done, x2_ready, x2_stats, x2_var, ve2_ready, x2_rstd, x2n_ready, x2b_ready = (
            sem("o_done"), sem("x2_ready"), sem("x2_stats"), sem("x2_var"), sem("ve2_ready"), sem("x2_rstd"), sem("x2n_ready"), sem("x2b_ready"))
        x2_hi, x2_lo, x2T_turned, f_done, out_ready = (
            sem("x2_hi"), sem("x2_lo"), sem("x2T_turned"), sem("f_done"), sem("out_ready"))

        block = stack.enter_context(nc.Block())

        def tile(q, b, lag):
            return q + (b + lag) // B, (b + lag) % B

        def valid(q):
            return not isinstance(q, int) or 0 <= q < NQ

        def nth(q, b, per=1):
            return q * (B * per) + b * per

        def positive(q, b, back):
            return not isinstance(q, int) or q * B + b - back >= 0

        def steps(eng, step):
            for n in range(-1, FIRST):
                step(*tile(0, 0, n))
            with eng.Fori(FIRST // B, FIRST // B + LOOPS) as q:
                for n in range(B):
                    step(*tile(q, FIRST % B, n))
            for n in range(FIRST + LOOPS * B, NT + 3):
                step(*tile(0, 0, n))

        @block.sync
        def _(sp):
            sp.dma_start(ctx_raw, ctx_in.rearrange("b j d -> j b d")).then_inc(ctx_loaded, 16)
            sp.dma_start(wk_raw, wk.rearrange("(k p) n -> p k n", p=P)).then_inc(wk_loaded, 16)
            sp.dma_start(wq_raw, wq.rearrange("(k p) n -> p k n", p=P)).then_inc(wq_loaded, 16)
            sp.dma_start(wv_raw, wv.rearrange("(k p) n -> p k n", p=P)).then_inc(wv_loaded, 16)
            sp.wait_ge(idx_ready, 1)
            op = sp.value_load(pick_idx[0:1, 0:1], min_val=0, max_val=NOPS - 1)
            sp.dma_start(wf_raw, ffn_w[bass.ds(op, 1), :, :].rearrange("o (k p) n -> p (o k) n", p=P)).then_inc(wf_loaded, 16)
            sp.wait_ge(wf_lo, 1)
            sp.wait_ge(wf_hi, 1)
            sp.dma_start(wo_raw, wo.rearrange("(h p) n -> p h n", p=P)).then_inc(wo_loaded, 16)
            sp.wait_ge(vw_lo, B * KT * NG)
            sp.dma_start(xin[:, 0, :], x[0, 0:P, :]).then_inc(x_loaded[0], 16)
            sp.dma_start(xin[:, 1, :], x[1, 0:P, :]).then_inc(x_loaded[1], 16)
            sp.dma_start(bias[:, 0, :], bo.rearrange("(a n) -> a n", a=1).to_broadcast([P, D])).then_inc(bias_loaded, 16)
            sp.dma_start(bias[:, 1, :], ffn_b[bass.ds(op, 1), :].to_broadcast([P, D])).then_inc(bias_loaded, 16)

            def due(semaphore, count):
                sp.wait_ge(semaphore, count)
                sp.sem_inc(turn_due, 1)

            def step(q, b):
                q1, b1 = tile(q, b, 1)
                q2, b2 = tile(q, b, -2)
                q3, b3 = tile(q, b, -3)
                ql, bl = tile(q, b, 3)
                if valid(q3):
                    sp.wait_ge(out_ready, nth(q3, b3) + 1)
                    sp.dma_start(out[b3, bass.ds(q3 * P, P), :], outb[:, b3 % 2, :]).then_inc(out_stored[b3 % 2], 16)
                if valid(q2):
                    if positive(q2, b2, 1):
                        due(f_done, nth(q2, b2))
                    due(x2_lo, nth(q2, b2) + 1)
                    sp.dma_start_transpose(x2T.rearrange("p s k n -> p (s k) n"),
                                           x2s.rearrange("p s n -> p (s n)")).then_inc(x2T_turned, 16)
                if valid(q1):
                    due(x_lo, nth(q1, b1) + 1)
                    if positive(q1, b1, 1):
                        due(s_done, nth(q1, b1, len(BANKS)))
                    sp.dma_start_transpose(xT.rearrange("p s k n -> p (s k) n"),
                                           xs.rearrange("p s n -> p (s n)")).then_inc(xT_turned, 16)
                if valid(ql):
                    sp.wait_ge(res_ready, nth(ql, bl) - 1)
                    sp.dma_start(xin[:, bl % 2, :], x[bl, bass.ds(ql * P, P), :]).then_inc(x_loaded[bl % 2], 16)
                if valid(q):
                    if positive(q, b, 1):
                        due(o_done, nth(q, b))
                    else:
                        sp.wait_ge(pad_zeroed, 1)
                    due(p_lo, nth(q, b) + 1)
                    sp.dma_start_transpose(pT.rearrange("p s c n -> p (s c) n"),
                                           ps.rearrange("p s n -> p (s n)")).then_inc(pT_turned, 16)

            steps(sp, step)
            for r in range(2):
                sp.wait_ge(out_stored[r], 16 * (NT // 2))

        @block.gpsimd
        def _(pool):
            nc.gpsimd.memset(ident[:, :], 0.0).then_inc(ident_zero, 1)
            pool.wait_ge(ident_zero, 1)
            nc.gpsimd.affine_select(out=ident[:, :], in_=ident[:, :], compare_op=ALU.not_equal, fill=1.0, base=0,
                                    pattern=[[-1, P]], channel_multiplier=1).then_inc(ident_ready, 1)
            nc.gpsimd.memset(neg_half, -0.5).then_inc(consts_set, 1)
            nc.gpsimd.memset(eps, EPS).then_inc(consts_set, 1)
            pool.wait_ge(consts_set, 2)
            nc.gpsimd.memset(diag[:, :, :, :, :].rearrange("p s h e n -> p (s h e n)").bitcast(U32), 0).then_inc(diag_zeroed, 1)
            for n, k in enumerate((WQ, KK, WF, VV, WO)):
                pool.wait_ge(amax_ready, n + 1)
                nc.gpsimd.partition_all_reduce(amax_all[:, k:k + 1], amax[:, k:k + 1], P,
                                               bass.bass_isa.ReduceOp.max).then_inc(amax_shared, 1)
            pool.wait_ge(vw_lo, B * KT * NG)

            nc.gpsimd.memset(ps[:, :, HJ:NC * P], 0.0).then_inc(pad_zeroed, 1)

            def step(q, b):
                q1, b1 = tile(q, b, 1)
                q2, b2 = tile(q, b, -2)
                if valid(q2):
                    pool.wait_ge(x2_var, nth(q2, b2) + 1)
                    nc.gpsimd.tensor_tensor(ve2, mv2[:, 1:2], eps, ALU.add).then_inc(ve2_ready, 1)
                    pool.wait_ge(ve2_ready, nth(q2, b2) + 1)
                    nc.gpsimd.tensor_tensor(rstd2, ve2, neg_half, ALU.pow).then_inc(x2_rstd, 1)
                if valid(q1):
                    pool.wait_ge(x_var, nth(q1, b1) + 1)
                    nc.gpsimd.tensor_tensor(ve1, mv1[:, 1:2], eps, ALU.add).then_inc(ve1_ready, 1)
                    pool.wait_ge(ve1_ready, nth(q1, b1) + 1)
                    nc.gpsimd.tensor_tensor(rstd1, ve1, neg_half, ALU.pow).then_inc(x_rstd, 1)
                    if isinstance(q, int) and nth(q1, b1) == 0:
                        pool.wait_ge(bias_loaded, 32)
                        for k in range(2):
                            nc.gpsimd.tensor_scalar(bias[:, k, :], bias[:, k, :], gates[:, k:k + 1], None, ALU.mult).then_inc(bias_ready, 1)
                        pool.wait_ge(bias_ready, 2)
                    if positive(q1, b1, 4):
                        pool.wait_ge(out_ready, nth(q1, b1) - 3)
                    nc.gpsimd.tensor_tensor(res[:, b1, :], xin[:, b1 % 2, :], bias[:, 0, :], ALU.add).then_inc(res_ready, 1)
                if valid(q2):
                    pool.wait_ge(x2n_ready, nth(q2, b2) + 1)
                    nc.gpsimd.tensor_tensor(res[:, b2, :], res[:, b2, :], bias[:, 1, :], ALU.add).then_inc(x2b_ready, 1)

            steps(pool, step)

        @block.scalar
        def _(act):
            act.dma_start(pick[0:1, 0:NOPS], logits.rearrange("(a n) -> a n", a=1)).then_inc(small_loaded, 16)
            act.dma_start(pick[0:1, 8:8 + NOPS], u.rearrange("(a n) -> a n", a=1)).then_inc(small_loaded, 16)
            act.dma_start(gate_in[:, 0:1], g_xattn.rearrange("(a n) -> a n", a=1).to_broadcast([P, 1])).then_inc(small_loaded, 16)
            act.dma_start(gate_in[:, 1:2], g_ffn.rearrange("(a n) -> a n", a=1).to_broadcast([P, 1])).then_inc(small_loaded, 16)
            act.wait_ge(small_loaded, 64)
            nc.scalar.activation(gates, gate_in, ACT.Tanh).then_inc(gate_ready, 1)
            act.wait_ge(pick_step, 2)
            nc.scalar.activation(pick[0:1, 24:32], pick[0:1, 16:24], ACT.Exp, accum_out=pick[0:1, 32:33]).then_inc(pick_step, 1)
            act.wait_ge(pick_step, 3)
            nc.scalar.activation(pick[0:1, 33:34], pick[0:1, 32:33], ACT.Ln).then_inc(pick_step, 1)
            nc.scalar.activation(pick[0:1, 40:48], pick[0:1, 8:16], ACT.Ln).then_inc(pick_step, 1)
            act.wait_ge(pick_step, 5)
            nc.scalar.activation(pick[0:1, 48:56], pick[0:1, 40:48], ACT.Ln, scale=-1.0).then_inc(pick_step, 1)

            for b in range(B):
                act.wait_ge(ctxT_done, b + 1)
                nc.scalar.copy(ctxT[:, :, b * J:(b + 1) * J],
                               banks[:, b, 0:CT * J].rearrange("p (k n) -> p k n", k=CT)).then_inc(ctxT_copied, 1)
            for h in range(HP):
                act.wait_ge(k_done, h + 1)
                nc.scalar.copy(kvT[:, h, :], banks[:, h, 0:BJ]).then_inc(k_copied, 1)
            act.wait_ge(scale_ready, 1)
            for h in range(HP):
                act.wait_ge(wqT_done, h + 1)
                nc.scalar.activation(wqT[:, 0, h, :], banks[:, h, :], ACT.Copy, scale=scl[:, WQ:WQ + 1]).then_inc(wqT_hi, 1)

            def diagonal_hi(k, done):
                for e in range(2):
                    rows = slice(DH * e, DH * e + DH)
                    nc.scalar.activation(diag[rows, 0, :, e, :], kvT[rows, :, :], ACT.Copy,
                                         scale=scl[rows, k:k + 1]).then_inc(done, 1)

            act.wait_ge(scale_ready, 2)
            act.wait_ge(diag_zeroed, 1)
            diagonal_hi(KK, k_hi)
            act.wait_ge(scale_ready, 3)
            act.wait_ge(wf_loaded, 16)
            nc.scalar.activation(wf_split[:, 0, :, :], wf_raw, ACT.Copy, scale=scl[:, WF:WF + 1]).then_inc(wf_hi, 1)
            with act.Fori(0, HP) as h:
                for e in range(2):
                    for k in range(KT):
                        act.wait_ge(a_done, h * (2 * KT) + (e * KT + k + 1))
                        nc.scalar.activation(
                            a_split[:, 0, k, :, bass.ds(h * (2 * J) + e * J, J)],
                            banks[:, e * KT + k, 0:BJ].rearrange("p (b n) -> p b n", b=B),
                            ACT.Copy, scale=2.0 ** FOLD_BITS).then_inc(a_hi, 1)
            for h in range(HP):
                act.wait_ge(v_done, h + 1)
                if h == 0:
                    act.wait_ge(k_lo, 2)
                nc.scalar.copy(kvT[:, h, :], banks[:, h, 0:BJ]).then_inc(v_copied, 1)
            act.wait_ge(scale_ready, 4)
            act.wait_ge(a_done, HEADS * KT)
            diagonal_hi(VV, v_hi)
            act.wait_ge(scale_ready, 5)
            act.wait_ge(ctxT_done, B)
            nc.scalar.activation(wo_split[:, 0, :, :], wo_raw, ACT.Copy, scale=scl[:, WO:WO + 1]).then_inc(wo_hi, 1)
            act.wait_ge(wo_lo, 1)
            with act.Fori(0, KT) as t:
                for h in range(0, HEADS, 2):
                    act.wait_ge(vwT_done, t * HEADS + (h + 1))
                    nc.scalar.copy(vwT[:, :, h * J:(h + 1) * J],
                                   banks[:, h % 8, 0:BJ].rearrange("p (b n) -> p b n", b=B)).then_inc(vwT_even, 1)
                for n in range(B * NG):
                    b, g = n // NG, n % NG
                    cs = GROUPS[g]
                    act.wait_ge(vw_done, t * (B * NG) + (n + 1))
                    nc.scalar.activation(vw[:, b, 0, cs.start:cs.stop, bass.ds(t * P, P)],
                                         banks[:, n % 8, 0:len(cs) * P].rearrange("p (c n) -> p c n", n=P),
                                         ACT.Copy, scale=2.0 ** FOLD_BITS).then_inc(vw_hi, 1)

            act.wait_ge(loop_scales, 3)

            def step(q, b):
                q1, b1 = tile(q, b, 1)
                q2, b2 = tile(q, b, -2)
                if valid(q2):
                    act.wait_ge(x2n_ready, nth(q2, b2) + 1)
                    if positive(q2, b2, 1):
                        act.wait_ge(x2T_turned, nth(q2, b2, 16))
                    nc.scalar.activation(x2s[:, 0, :], x2n, ACT.Copy, scale=2.0 ** XN_BITS).then_inc(x2_hi, 1)
                if valid(q):
                    act.wait_ge(shifted, nth(q, b, len(BANKS)) + 1)
                    exponentials(0)
                if valid(q1):
                    act.wait_ge(xn_ready, nth(q1, b1) + 1)
                    if positive(q1, b1, 1):
                        act.wait_ge(xT_turned, nth(q1, b1, 16))
                    nc.scalar.activation(xs[:, 0, :], xn, ACT.Copy, scale=2.0 ** XN_BITS).then_inc(x_hi, 1)
                if valid(q):
                    for k in range(1, len(BANKS)):
                        act.wait_ge(shifted, nth(q, b, len(BANKS)) + k + 1)
                        exponentials(k)
                    act.wait_ge(p_ready, nth(q, b) + 1)
                    if positive(q, b, 1):
                        act.wait_ge(pT_turned, nth(q, b, 16))
                    else:
                        act.wait_ge(pad_zeroed, 1)
                    nc.scalar.activation(ps[:, 0, 0:HJ], probs, ACT.Copy, scale=2.0 ** PROB_BITS).then_inc(p_hi, 1)

            def exponentials(k):
                cols = slice(BANKS[k][0] * J, BANKS[k][1] * J)
                nc.scalar.activation(probs[:, cols], probs[:, cols], ACT.Exp, scale=exp_scale).then_inc(exp_done, 1)

            steps(act, step)

        @block.vector
        def _(dve):
            lg, uu, sh = pick[0:1, 0:8], pick[0:1, 8:16], pick[0:1, 16:24]
            dve.wait_ge(small_loaded, 64)
            nc.vector.reduce_max(pick[0:1, 34:35], lg, AX.X).then_inc(pick_step, 1)
            dve.wait_ge(pick_step, 1)
            nc.vector.tensor_scalar(sh, lg, pick[0:1, 34:35], None, ALU.subtract).then_inc(pick_step, 1)
            dve.wait_ge(pick_step, 6)
            nc.vector.tensor_scalar(pick[0:1, 56:64], sh, pick[0:1, 33:34], None, ALU.subtract).then_inc(pick_step, 1)
            dve.wait_ge(pick_step, 7)
            nc.vector.tensor_tensor(pick[0:1, 64:72], pick[0:1, 56:64], pick[0:1, 48:56], ALU.subtract).then_inc(pick_step, 1)
            dve.wait_ge(pick_step, 8)
            nc.vector.max(pick[0:1, 72:80], pick[0:1, 64:72]).then_inc(pick_step, 1)
            dve.wait_ge(pick_step, 9)
            nc.vector.max_index(pick_idx[0:1, :], pick[0:1, 72:80], pick[0:1, 64:72]).then_inc(idx_ready, 1)

            count = [0]

            def power_of_two_scale(k, data, axis, bits):
                n = count[0] = count[0] + 1
                nc.vector.tensor_reduce(amax[:, k:k + 1], data, axis, ALU.max, apply_absolute_value=True).then_inc(amax_ready, 1)
                dve.wait_ge(amax_shared, n)
                nc.vector.tensor_scalar(amax[:, k:k + 1], amax_all[:, k:k + 1], 1e-30, None, ALU.max).then_inc(pow2_ready, 1)
                dve.wait_ge(pow2_ready, 3 * n - 2)
                nc.vector.tensor_scalar(pow2[:, k:k + 1].bitcast(U32), amax[:, k:k + 1].bitcast(U32), 0x7F800000, None,
                                        ALU.bitwise_and).then_inc(pow2_ready, 1)
                dve.wait_ge(pow2_ready, 3 * n - 1)
                nc.vector.tensor_scalar(pow2[:, k:k + 1], pow2[:, k:k + 1], 2.0 ** -bits, None, ALU.mult).then_inc(pow2_ready, 1)
                dve.wait_ge(pow2_ready, 3 * n)
                nc.vector.reciprocal(scl[:, k:k + 1], pow2[:, k:k + 1]).then_inc(scale_ready, 1)
                dve.wait_ge(scale_ready, n)

            def low(lo, value, scale, hi):
                return nc.vector.scalar_tensor_tensor(out=lo, in0=value, scalar=scale, in1=hi, op0=ALU.mult, op1=ALU.subtract)

            def diagonal_lo(k, hi_ready, done):
                for e in range(2):
                    rows = slice(DH * e, DH * e + DH)
                    dve.wait_ge(hi_ready, e + 1)
                    low(diag[rows, 1, :, e, :], kvT[rows, :, :], scl[rows, k:k + 1], diag[rows, 0, :, e, :]).then_inc(done, 1)

            dve.wait_ge(wq_loaded, 16)
            power_of_two_scale(WQ, wq_raw, AX.XY, OPERAND_BITS)
            dve.wait_ge(k_copied, HP)
            power_of_two_scale(KK, kvT, AX.XY, OPERAND_BITS)
            for h in range(HP):
                dve.wait_ge(wqT_hi, h + 1)
                low(wqT[:, 1, h, :], banks[:, h, :], scl[:, WQ:WQ + 1], wqT[:, 0, h, :]).then_inc(wqT_lo, 1)
            diagonal_lo(KK, k_hi, k_lo)
            dve.wait_ge(wf_loaded, 16)
            power_of_two_scale(WF, wf_raw, AX.XY, WF_BITS)
            dve.wait_ge(wf_hi, 1)
            low(wf_split[:, 1, :, :].rearrange("p k n -> p (k n)"), wf_raw.rearrange("p k n -> p (k n)"), scl[:, WF:WF + 1],
                wf_split[:, 0, :, :].rearrange("p k n -> p (k n)")).then_inc(wf_lo, 1)
            with dve.Fori(0, HP) as h:
                for e in range(2):
                    for k in range(KT):
                        dve.wait_ge(a_hi, h * (2 * KT) + (e * KT + k + 1))
                        low(a_split[:, 1, k, :, bass.ds(h * (2 * J) + e * J, J)],
                            banks[:, e * KT + k, 0:BJ].rearrange("p (b n) -> p b n", b=B), 2.0 ** FOLD_BITS,
                            a_split[:, 0, k, :, bass.ds(h * (2 * J) + e * J, J)]).then_inc(a_lo, 1)
            dve.wait_ge(v_copied, HP)
            power_of_two_scale(VV, kvT, AX.XY, OPERAND_BITS)
            diagonal_lo(VV, v_hi, v_lo)
            dve.wait_ge(wo_loaded, 16)
            power_of_two_scale(WO, wo_raw, AX.XY, OPERAND_BITS)
            dve.wait_ge(wo_hi, 1)
            low(wo_split[:, 1, :, :].rearrange("p k n -> p (k n)"), wo_raw.rearrange("p k n -> p (k n)"), scl[:, WO:WO + 1],
                wo_split[:, 0, :, :].rearrange("p k n -> p (k n)")).then_inc(wo_lo, 1)

            back = [2.0 ** (-FOLD_BITS - XN_BITS) * DH ** -0.5, 2.0 ** (-FOLD_BITS - PROB_BITS), 2.0 ** -XN_BITS]
            dve.wait_ge(gate_ready, 1)
            nc.vector.scalar_tensor_tensor(out=exp_scale, in0=pow2[:, KK:KK + 1], scalar=back[0], in1=pow2[:, WQ:WQ + 1],
                                           op0=ALU.mult, op1=ALU.mult).then_inc(loop_scales, 1)
            nc.vector.scalar_tensor_tensor(out=amax[:, 7:8], in0=pow2[:, VV:VV + 1], scalar=back[1], in1=pow2[:, WO:WO + 1],
                                           op0=ALU.mult, op1=ALU.mult).then_inc(loop_scales, 1)
            nc.vector.scalar_tensor_tensor(out=f_scale, in0=pow2[:, WF:WF + 1], scalar=back[2], in1=gates[:, 1:2],
                                           op0=ALU.mult, op1=ALU.mult).then_inc(loop_scales, 1)
            dve.wait_ge(loop_scales, 3)
            nc.vector.tensor_tensor(o_scale, amax[:, 7:8], gates[:, 0:1], ALU.mult).then_inc(loop_scales, 1)

            with dve.Fori(0, KT) as t:
                for h in range(1, HEADS, 2):
                    dve.wait_ge(vwT_done, t * HEADS + (h + 1))
                    nc.vector.tensor_copy(vwT[:, :, h * J:(h + 1) * J],
                                          banks[:, h % 8, 0:BJ].rearrange("p (b n) -> p b n", b=B)).then_inc(vwT_odd, 1)
                for n in range(B * NG):
                    b, g = n // NG, n % NG
                    cs = GROUPS[g]
                    dve.wait_ge(vw_hi, t * (B * NG) + (n + 1))
                    low(vw[:, b, 1, cs.start:cs.stop, bass.ds(t * P, P)],
                        banks[:, n % 8, 0:len(cs) * P].rearrange("p (c n) -> p c n", n=P), 2.0 ** FOLD_BITS,
                        vw[:, b, 0, cs.start:cs.stop, bass.ds(t * P, P)]).then_inc(vw_lo, 1)

            dve.wait_ge(loop_scales, 4)
            dve.wait_ge(vw_lo, B * KT * NG)

            NB = len(BANKS)

            def by_head(ap):
                return ap.rearrange("p (h n) -> p h n", n=J)

            def step(q, b):
                q1, b1 = tile(q, b, 1)
                qp, bp = tile(q, b, -1)
                q2, b2 = tile(q, b, -2)
                q3, b3 = tile(q, b, -3)

                def maxima(k):
                    h0, h1 = BANKS[k]
                    dve.wait_ge(s_done, nth(q, b, NB) + k + 1)
                    nc.vector.reduce_max(mx[:, h0:h1], by_head(s_ps[:, k, 0:(h1 - h0) * J]), AX.X).then_inc(mx_ready, 1)

                def shift(k):
                    h0, h1 = BANKS[k]
                    dve.wait_ge(mx_ready, nth(q, b, NB) + k + 1)
                    nc.vector.tensor_tensor(by_head(probs[:, h0 * J:h1 * J]), by_head(s_ps[:, k, 0:(h1 - h0) * J]),
                                            mx[:, h0:h1].unsqueeze(2).to_broadcast([P, h1 - h0, J]), ALU.subtract).then_inc(shifted, 1)

                if valid(q2):
                    dve.wait_ge(x2_stats, nth(q2, b2) + 1)
                if valid(q3):
                    dve.wait_ge(f_done, nth(q3, b3) + 1)
                    dve.wait_ge(x2b_ready, nth(q3, b3) + 1)
                    if positive(q3, b3, 2):
                        dve.wait_ge(out_stored[b3 % 2], (q3 * 2 + b3 // 2) * 16)
                    nc.vector.scalar_tensor_tensor(out=outb[:, b3 % 2, :], in0=f_ps, scalar=f_scale, in1=res[:, b3, :],
                                                   op0=ALU.mult, op1=ALU.add).then_inc(out_ready, 1)
                if valid(q1):
                    dve.wait_ge(x_loaded[b1 % 2], (q1 * 2 + b1 // 2 + 1) * 16)
                    nc.vector.bn_stats(bn1, xin[:, b1 % 2, :]).then_inc(x_stats, 1)
                if valid(q2):
                    nc.vector.bn_aggr(mv2, bn2).then_inc(x2_var, 1)
                if valid(q1):
                    dve.wait_ge(x_stats, nth(q1, b1) + 1)
                if valid(q):
                    maxima(0)
                if valid(q1):
                    nc.vector.bn_aggr(mv1, bn1).then_inc(x_var, 1)
                if valid(q):
                    shift(0)
                if valid(q2):
                    dve.wait_ge(x2_rstd, nth(q2, b2) + 1)
                    nc.vector.tensor_scalar(x2n, res[:, b2, :], mv2[:, 0:1], rstd2, ALU.subtract, ALU.mult).then_inc(x2n_ready, 1)
                if valid(q):
                    maxima(1)
                if valid(q1):
                    dve.wait_ge(x_rstd, nth(q1, b1) + 1)
                    nc.vector.tensor_scalar(xn, xin[:, b1 % 2, :], mv1[:, 0:1], rstd1, ALU.subtract, ALU.mult).then_inc(xn_ready, 1)
                if valid(q):
                    shift(1)
                if valid(q2):
                    dve.wait_ge(x2_hi, nth(q2, b2) + 1)
                    low(x2s[:, 1, :], x2n, 2.0 ** XN_BITS, x2s[:, 0, :]).then_inc(x2_lo, 1)
                if valid(q):
                    maxima(2)
                if valid(q1):
                    dve.wait_ge(x_hi, nth(q1, b1) + 1)
                    low(xs[:, 1, :], xn, 2.0 ** XN_BITS, xs[:, 0, :]).then_inc(x_lo, 1)
                if valid(q):
                    shift(2)
                    dve.wait_ge(exp_done, nth(q, b, NB) + NB)
                    nc.vector.reduce_sum(sums, by_head(probs), AX.X).then_inc(sum_ready, 1)
                    dve.wait_ge(sum_ready, nth(q, b) + 1)
                    nc.vector.reciprocal(rsum, sums).then_inc(rsum_ready, 1)
                    dve.wait_ge(rsum_ready, nth(q, b) + 1)
                    nc.vector.tensor_tensor(by_head(probs), by_head(probs),
                                            rsum.unsqueeze(2).to_broadcast([P, HEADS, J]), ALU.mult).then_inc(p_ready, 1)
                    dve.wait_ge(p_hi, nth(q, b) + 1)
                    low(ps[:, 1, 0:HJ], probs, 2.0 ** PROB_BITS, ps[:, 0, 0:HJ]).then_inc(p_lo, 1)
                if valid(qp):
                    dve.wait_ge(o_done, nth(qp, bp) + 1)
                    dve.wait_ge(res_ready, nth(qp, bp) + 1)
                    nc.vector.scalar_tensor_tensor(out=res[:, bp, :], in0=o_ps, scalar=o_scale, in1=res[:, bp, :],
                                                   op0=ALU.mult, op1=ALU.add).then_inc(x2_ready, 1)
                    dve.wait_ge(x2_ready, nth(qp, bp) + 1)
                    nc.vector.bn_stats(bn2, res[:, bp, :]).then_inc(x2_stats, 1)

            steps(dve, step)

        @block.tensor
        def _(pe):
            def split_products(ps, lhs, rhs, first, last):
                for n, (l, r) in enumerate(((0, 0), (0, 1), (1, 0))):
                    mm = nc.tensor.matmul(ps, lhs(l), rhs(r), start=first and n == 0, stop=last and n == 2)
                return mm

            pe.wait_ge(ident_ready, 1)
            pe.wait_ge(ctx_loaded, 16)
            for b in range(B):
                for k in range(CT):
                    mm = nc.tensor.transpose(banks[:, b, k * J:(k + 1) * J], ctx_raw[:, b, k * P:(k + 1) * P], ident[0:J, 0:J])
                mm.then_inc(ctxT_done, 1)
            pe.wait_ge(wk_loaded, 16)
            pe.wait_ge(ctxT_copied, B)
            for h in range(HP):
                for k in range(CT):
                    mm = nc.tensor.matmul(banks[:, h, 0:BJ], wk_raw[:, k, h * P:(h + 1) * P], ctxT[:, k, :],
                                          start=k == 0, stop=k == CT - 1)
                mm.then_inc(k_done, 1)
            pe.wait_ge(wq_loaded, 16)
            for h in range(HP):
                pe.wait_ge(k_copied, h + 1)
                for k in range(KT):
                    mm = nc.tensor.transpose(banks[:, h, k * P:(k + 1) * P], wq_raw[:, k, h * P:(h + 1) * P], ident[:, :])
                mm.then_inc(wqT_done, 1)
            pe.wait_ge(wqT_lo, HP)
            pe.wait_ge(k_lo, 2)

            def fold_k(h):
                for e in range(2):
                    for k in range(KT):
                        if not isinstance(h, int):
                            pe.wait_ge(a_lo, h * (2 * KT) + (e * KT + k + 1 - 2 * KT))
                        split_products(banks[:, e * KT + k, 0:BJ],
                                       lambda s: wqT[:, s, bass.ds(h, 1), k * P:(k + 1) * P].rearrange("p o n -> p (o n)"),
                                       lambda s: diag[:, s, bass.ds(h, 1), e, :].rearrange("p o n -> p (o n)"),
                                       True, True).then_inc(a_done, 1)

            fold_k(0)
            with pe.Fori(1, HP) as h:
                fold_k(h)
            pe.wait_ge(wv_loaded, 16)
            pe.wait_ge(a_lo, HEADS * KT)
            for h in range(HP):
                for k in range(CT):
                    mm = nc.tensor.matmul(banks[:, h, 0:BJ], wv_raw[:, k, h * P:(h + 1) * P], ctxT[:, k, :],
                                          start=k == 0, stop=k == CT - 1)
                mm.then_inc(v_done, 1)
            pe.wait_ge(v_copied, HP)
            pe.wait_ge(v_lo, 2)
            pe.wait_ge(wo_lo, 1)
            with pe.Fori(0, KT) as t:
                for h in range(HEADS):
                    if h < 8:
                        pass
                    elif h % 2 == 0:
                        pe.wait_ge(vwT_even, t * HP + (h - 8) // 2 + 1)
                    else:
                        pe.wait_ge(vwT_odd, t * HP + (h - 8) // 2 + 1)
                    split_products(banks[:, h % 8, 0:BJ],
                                   lambda s: wo_split[:, s, h // 2, bass.ds(t * P, P)],
                                   lambda s: diag[:, s, h // 2, h % 2, :], True, True).then_inc(vwT_done, 1)
                pe.wait_ge(vwT_even, t * HP + HP)
                pe.wait_ge(vwT_odd, t * HP + HP)
                for n in range(B * NG):
                    b, g = n // NG, n % NG
                    if n >= 8:
                        pe.wait_ge(vw_lo, t * (B * NG) + (n - 7))
                    for m, ch in enumerate(GROUPS[g]):
                        lo, hi = CHUNKS[ch]
                        mm = nc.tensor.transpose(banks[0:hi - lo, n % 8, m * P:(m + 1) * P], vwT[:, b, lo:hi], ident[:, :])
                    mm.then_inc(vw_done, 1)
                pe.wait_ge(vw_lo, t * (B * NG) + B * NG)
            pe.wait_ge(wf_lo, 1)

            def step(q, b):
                qp, bp = tile(q, b, -1)
                q2, b2 = tile(q, b, -2)
                if valid(q):
                    pe.wait_ge(xT_turned, nth(q, b, 16) + 16)
                    if positive(q, b, 1):
                        pe.wait_ge(shifted, nth(q, b, len(BANKS)))
                    for n, (h0, h1) in enumerate(BANKS):
                        for k in range(KT):
                            mm = split_products(s_ps[:, n, 0:(h1 - h0) * J], lambda s: xT[:, s, k, :],
                                                lambda s: a_split[:, s, k, b, h0 * J:h1 * J], k == 0, k == KT - 1)
                        mm.then_inc(s_done, 1)
                if valid(qp):
                    pe.wait_ge(pT_turned, nth(qp, bp, 16) + 16)
                    if positive(qp, bp, 1):
                        pe.wait_ge(x2_ready, nth(qp, bp))
                    for ch, (lo, hi) in enumerate(CHUNKS):
                        mm = split_products(o_ps, lambda s: pT[0:hi - lo, s, ch, :], lambda s: vw[0:hi - lo, bp, s, ch, :],
                                            ch == 0, ch == NC - 1)
                    mm.then_inc(o_done, 1)
                if valid(q2):
                    pe.wait_ge(x2T_turned, nth(q2, b2, 16) + 16)
                    if positive(q2, b2, 1):
                        pe.wait_ge(out_ready, nth(q2, b2))
                    for k in range(KT):
                        mm = split_products(f_ps, lambda s: x2T[:, s, k, :], lambda s: wf_split[:, s, k, :], k == 0, k == KT - 1)
                    mm.then_inc(f_done, 1)

            steps(pe, step)


_INS = ["x", "ctx_768", "g_xattn", "g_ffn", "L0_xattn_Wq", "L0_xattn_Wk", "L0_xattn_Wv", "L0_xattn_Wo", "L0_xattn_bo",
        "L0_ffn_W", "L0_ffn_b", "L0_ffn_logits", "L0_ffn_u"]


def kernel(**inputs):
    import numpy as np
    import concourse.bacc as bacc
    from concourse import mybir as mb
    from concourse.bass_utils import run_bass_kernel_spmd

    nc = bacc.Bacc("TRN2", target_bir_lowering=False, num_devices=1, dynamic_dma_scratch_size=1024)
    arrays, args = {}, []
    for name in _INS:
        a = np.ascontiguousarray(inputs[name])
        arrays[f"in_{name}"] = a
        args.append(nc.dram_tensor(f"in_{name}", a.shape, mb.dt.from_np(a.dtype), kind="ExternalInput").ap())
    shape = inputs["x"].shape
    args.append(nc.dram_tensor("out_0", shape, mb.dt.float32, kind="ExternalOutput").ap())
    flamingo_layer(nc, *args)
    r = run_bass_kernel_spmd(nc, [arrays], core_ids=[0])
    return r.results[0]["out_0"]
```

```python
from contextlib import ExitStack

import concourse.bass as bass
from concourse import mybir

ALU = mybir.AluOpType
ACT = mybir.ActivationFunctionType
AX = mybir.AxisListType
F32 = mybir.dt.float32
F16 = mybir.dt.float16
U32 = mybir.dt.uint32

P = 128
HEADS = 16
DH = 64
EPS = 1e-5
OPERAND_BITS = 10
FOLD_BITS = -13
XN_BITS = 8
PROB_BITS = 14
WF_BITS = 13


def flamingo_layer(nc, x, ctx_in, g_xattn, g_ffn, wq, wk, wv, wo, bo, ffn_w, ffn_b, logits, u, out):
    B, SQ, D = x.shape
    _, J, CD = ctx_in.shape
    ID = HEADS * DH
    HJ = HEADS * J
    NOPS = ffn_w.shape[0]
    KT = D // P
    CT = CD // P
    HP = ID // P
    BJ = B * J
    NQ = SQ // P
    NC = -(-HJ // P)
    BODY = (NC - 1) * P
    TAIL = HJ - BODY
    TH = TAIL // 2
    LOW = NC * P
    KEYS = 2 * NC * P
    assert TAIL % 2 == 0 and TAIL + TH <= P
    HB = 512 // J
    BANKS = [(h, min(h + HB, HEADS)) for h in range(0, HEADS, HB)]
    NT = B * NQ
    FIRST = 6
    LOOPS = (NT - 3 - FIRST) // B
    assert B == 4 and D == 512 and len(BANKS) == 3

    with ExitStack() as stack:
        def sb(name, shape, dt=F32):
            return stack.enter_context(nc.sbuf_tensor(name, shape, dt))

        def sem(name):
            return stack.enter_context(nc.semaphore(name))

        A_WORDS = KT * B * HJ
        VW_WORDS = KT * B * KEYS // 2
        SLOT_WORDS = B * KEYS // 2
        DIAG_WORDS = 2 * BJ * HP
        LOOP_WORDS = SLOT_WORDS + DIAG_WORDS + HP * D
        big = sb("big", [P, A_WORDS + LOOP_WORDS])
        a_split = big[:, 0:A_WORDS].bitcast(F16).rearrange("p (k s b n) -> p k s b n", s=2, k=KT, b=B)
        arena = big[:, A_WORDS:A_WORDS + LOOP_WORDS]
        wf_area = sb("wf_area", [P, KT * D])
        wf_raw = wf_area[:, :].rearrange("p (k n) -> p k n", k=KT)
        xT_area = sb("xT_area", [P, D])
        vw_arena = sb("vw_arena", [P, VW_WORDS])
        vw = vw_arena[:, :].bitcast(F16).rearrange("p (t b c n) -> p t b c n", t=KT, b=B, n=P)
        cst = sb("cst", [P, 64])
        stats = sb("stats", [P, 64])

        class Carve:
            def __init__(self, base):
                self.base, self.at = base, 0

            def take(self, words):
                self.at += words
                return self.base[:, self.at - words:self.at]

        slots_at = A_WORDS - (KT - 1) * SLOT_WORDS
        slots = big[:, slots_at:A_WORDS + SLOT_WORDS].bitcast(F16).rearrange("p (t b n) -> p t b n", t=KT, b=B)
        assert HP * D <= slots_at
        wo_split = big[:, 0:HP * D].bitcast(F16).rearrange("p (s h n) -> p s h n", s=2, h=HP)
        c = Carve(big[:, slots_at:A_WORDS])
        vT = c.take(HP * BJ).rearrange("p (h n) -> p h n", h=HP)
        ctx_raw = c.take(B * CD)[0:J, :].rearrange("p (b n) -> p b n", b=B)
        wv_raw = c.take(CT * ID).rearrange("p (k n) -> p k n", k=CT)
        wk_raw = c.take(CT * ID).rearrange("p (k n) -> p k n", k=CT)
        assert c.at <= (KT - 1) * SLOT_WORDS
        c = Carve(vw_arena)
        wq_raw = c.take(KT * ID).rearrange("p (k n) -> p k n", k=KT)
        ctxT = c.take(CT * BJ).rearrange("p (k n) -> p k n", k=CT)
        assert c.at <= SLOT_WORDS
        c.at = SLOT_WORDS
        wo_raw = c.take(HP * D).rearrange("p (h n) -> p h n", h=HP)
        assert c.at <= (KT - 2) * SLOT_WORDS
        c.at = (KT - 2) * SLOT_WORDS
        kT = c.take(HP * BJ).rearrange("p (h n) -> p h n", h=HP)
        wo_scaled = vw_arena[:, c.at:c.at + ID].rearrange("p (h n) -> p h n", h=HP)
        k_scaled = c.take(HP * BJ).rearrange("p (h n) -> p h n", h=HP)
        ident = c.take(P)
        assert c.at <= (KT - 1) * SLOT_WORDS
        c.at = (KT - 1) * SLOT_WORDS + DIAG_WORDS
        pick = c.take(80)[0:1, :]
        pick_idx = c.take(8)[0:1, :].bitcast(U32)
        assert c.at <= VW_WORDS

        def blocks_of(words):
            return words.bitcast(F16).rearrange("p (s h b e n) -> p s h b e n", s=2, h=HP, b=B, e=2)

        v_diag = blocks_of(vw_arena[:, (KT - 1) * SLOT_WORDS:(KT - 1) * SLOT_WORDS + DIAG_WORDS])
        k_diag = blocks_of(arena[:, SLOT_WORDS:SLOT_WORDS + DIAG_WORDS])
        wqT = arena[:, SLOT_WORDS + DIAG_WORDS:LOOP_WORDS].bitcast(F16).rearrange("p (s h n) -> p s h n", s=2, h=HP)

        c = Carve(arena)
        xin = c.take(2 * D).rearrange("p (r n) -> p r n", r=2)
        xn = c.take(D)
        xs = c.take(D).bitcast(F16).rearrange("p (s n) -> p s n", s=2)
        xT = xT_area[:, :].bitcast(F16).rearrange("p (s k n) -> p s k n", s=2, k=KT)
        x2n = c.take(D)
        x2s = c.take(D).bitcast(F16).rearrange("p (s n) -> p s n", s=2)
        x2T = c.take(D).bitcast(F16).rearrange("p (s k n) -> p s k n", s=2, k=KT)
        outb = c.take(2 * D).rearrange("p (r n) -> p r n", r=2)
        assert c.at <= SLOT_WORDS
        c.at = SLOT_WORDS
        res = c.take(4 * D).rearrange("p (r n) -> p r n", r=4)
        probs = c.take(HJ)
        ps = c.take(KEYS // 2).bitcast(F16)
        pT = c.take(KEYS // 2).bitcast(F16).rearrange("p (c n) -> p c n", n=P)
        pT_last = big[:, 0:KEYS // 2].bitcast(F16).rearrange("p (c n) -> p c n", n=P)
        bias = c.take(2 * D).rearrange("p (k n) -> p k n", k=2)
        wf_split = c.take(KT * D).bitcast(F16).rearrange("p (s k n) -> p s k n", s=2, k=KT)
        assert c.at <= LOOP_WORDS, c.at

        amax, pow2, scl = cst[:, 0:8], cst[:, 8:16], cst[:, 16:24]
        WQ, VV, WO, KK, WF = range(5)
        amax_all = cst[:, 24:32]
        exp_scale, o_scale, f_scale = cst[:, 32:33], cst[:, 33:34], cst[:, 34:35]
        gates, gate_in = cst[:, 36:38], cst[:, 38:40]
        neg_half = cst[:, 40:41]
        eps = cst[:, 41:42]
        bn1, mv1, rstd1, ve1 = stats[:, 0:6], stats[:, 6:8], stats[:, 8:9], stats[:, 9:10]
        bn2, mv2, rstd2, ve2 = stats[:, 12:18], stats[:, 18:20], stats[:, 20:21], stats[:, 21:22]
        part_max, wo_max, wq_max, wf_max = cst[:, 60:64], stats[:, 56:58], stats[:, 58:60], stats[:, 60:64]
        mx, sums, rsum = stats[:, 24:40], stats[:, 40:56], cst[:, 44:60]

        banks = stack.enter_context(nc.psum_tensor("banks", [P, 8, 512], F32))
        s_ps = banks[:, 0:3, :]
        o_ps, f_ps = banks[:, 3, :], banks[:, 4, :]

        ctx_loaded = sem("ctx_loaded")
        wv_loaded, wo_loaded, wq_loaded, wk_loaded = ([sem(f"{w}_loaded{n}") for n in range(2)] for w in ("wv", "wo", "wq", "wk"))
        wf_loaded, small_loaded, gates_loaded, bias_loaded = sem("wf_loaded"), sem("small_loaded"), sem("gates_loaded"), sem("bias_loaded")
        ident_zero, ident_ready, diag_zeroed, pads_set = sem("ident_zero"), sem("ident_ready"), sem("diag_zeroed"), sem("pads_set")
        ctxT_done, ctxT_copied = sem("ctxT_done"), sem("ctxT_copied")
        k_done, k_copied, v_done, v_copied = sem("k_done"), sem("k_copied"), sem("v_done"), sem("v_copied")
        amax_ready, amax_shared, pow2_ready, scale_ready = sem("amax_ready"), sem("amax_shared"), sem("pow2_ready"), sem("scale_ready")
        wqT_done, wqT_hi, wqT_lo = sem("wqT_done"), sem("wqT_hi"), sem("wqT_lo")
        k_hi, k_lo, v_hi, v_lo = sem("k_hi"), sem("k_lo"), sem("v_hi"), sem("v_lo")
        wo_hi, wo_scaled_ready, wo_lo, wf_hi, wf_lo = sem("wo_hi"), sem("wo_scaled_ready"), sem("wo_lo"), sem("wf_hi"), sem("wf_lo")
        k_scaled_ready, wo_part, wq_part, wf_part, v_part, k_part = sem("k_scaled_ready"), sem("wo_part"), sem("wq_part"), sem("wf_part"), sem("v_part"), sem("k_part")
        a_done, a_hi, a_lo = sem("a_done"), sem("a_hi"), sem("a_lo")
        vwT_done, vwT_hi, vwT_tail, vwT_lo = sem("vwT_done"), sem("vwT_hi"), sem("vwT_tail"), sem("vwT_lo")
        vw_turned, vw_turned_end = [sem(f"vw_turned{t}") for t in range(KT)], sem("vw_turned_end")
        pick_step, idx_ready, gate_ready = sem("pick_step"), sem("idx_ready"), sem("gate_ready")
        exp_scale_ready, o_scale_ready, f_scale_ready, bias_ready = (
            sem("exp_scale_ready"), sem("o_scale_ready"), sem("f_scale_ready"), sem("bias_ready"))
        consts_set = sem("consts_set")
        x_loaded, x_first = [sem(f"x_loaded{r}") for r in range(2)], sem("x_first")
        turn_due = sem("turn_due")
        out_stored = [sem(f"out_stored{r}") for r in range(2)]
        x_stats, x_var, ve1_ready, x_rstd, xn_ready, res_ready = (
            sem("x_stats"), sem("x_var"), sem("ve1_ready"), sem("x_rstd"), sem("xn_ready"), sem("res_ready"))
        x_hi, x_lo, xT_turned = sem("x_hi"), sem("x_lo"), sem("xT_turned")
        s_done, mx_ready, shifted, exp_done = sem("s_done"), sem("mx_ready"), sem("shifted"), sem("exp_done")
        sum_ready, rsum_ready, p_ready, p_hi, p_lo, pT_turned, pad_zeroed = (
            sem("sum_ready"), sem("rsum_ready"), sem("p_ready"), sem("p_hi"), sem("p_lo"), sem("pT_turned"), sem("pad_zeroed"))
        p_tail, pT_parts = sem("p_tail"), [sem(f"pT_part{i}") for i in range(3)]
        o_done, x2_ready, x2_stats, x2_var, ve2_ready, x2_rstd, x2n_ready, x2b_ready = (
            sem("o_done"), sem("x2_ready"), sem("x2_stats"), sem("x2_var"), sem("ve2_ready"), sem("x2_rstd"), sem("x2n_ready"), sem("x2b_ready"))
        x2_hi, x2_lo, x2T_turned, f_done, out_ready = (
            sem("x2_hi"), sem("x2_lo"), sem("x2T_turned"), sem("f_done"), sem("out_ready"))

        block = stack.enter_context(nc.Block())

        def tile(q, b, lag):
            return q + (b + lag) // B, (b + lag) % B

        def valid(q):
            return not isinstance(q, int) or 0 <= q < NQ

        def nth(q, b, per=1):
            return q * (B * per) + b * per

        def positive(q, b, back):
            return not isinstance(q, int) or q * B + b - back >= 0

        def is_last(q, b):
            return isinstance(q, int) and q * B + b == NT - 1

        def pieces(q, b):
            alone = is_last(q, b) or not positive(q, b, 1)
            return [(0, 2), (2, 3)] if alone else [(0, 3)]

        EARLY = BANKS[1][1] * J // P

        def pieces_done(q, b, piece):
            return nth(q, b) + (1 if positive(q, b, 1) else 0) + pieces(q, b).index(piece) + 1

        def heads_of(piece):
            return BANKS[piece[0]][0], BANKS[piece[1] - 1][1]

        def probs_place(q, b):
            return pT_last if is_last(q, b) else pT

        def x2_place(q, b):
            return xT if is_last(q, b) else x2T

        def steps(eng, step):
            for n in range(FIRST):
                step(*tile(0, 0, n))
            with eng.Fori(FIRST // B, FIRST // B + LOOPS) as q:
                for n in range(B):
                    step(*tile(q, FIRST % B, n))
            for n in range(FIRST + LOOPS * B, NT + 3):
                step(*tile(0, 0, n))

        PW = 2 * J

        def half_pair(u):
            return banks[:, u % 8, :].rearrange("p (b n) -> p b n", b=2)[:, :, 0:PW]

        def pair_banks(h):
            return banks[:, 2 * h % 8:2 * h % 8 + 2, :].rearrange("p g (b n) -> p (g b) n", b=2)[:, :, 0:PW]

        def half_blocks(diag, s, h, g):
            return diag[:, s, h, 2 * g:2 * g + 2, :, :].rearrange("p b e n -> p (b e n)")

        def low_pieces(h):
            for start, stop, to in ((0, BODY, LOW), (BODY, BODY + TH, TAIL), (BODY + TH, HJ, LOW + TAIL - TH)):
                lo, hi = max(start, h * PW), min(stop, (h + 1) * PW)
                if lo < hi:
                    yield lo - h * PW, hi - h * PW, lo + to

        LOWS = [sum(len(list(low_pieces(g))) for g in range(h)) for h in range(HP + 1)]

        def slot(t, cols):
            return slots[:, bass.ds(t, 1), :, cols].rearrange("p o b n -> p (o b) n")

        def low(lo, value, scale, hi):
            return nc.vector.scalar_tensor_tensor(out=lo, in0=value, scalar=scale, in1=hi, op0=ALU.mult, op1=ALU.subtract)

        def one_head(diag, rows, s, e):
            return diag[rows, s, :, :, e, :].rearrange("p h b n -> p (h b) n")

        def by_batch(data, rows):
            return data[rows, :, :].rearrange("p h (b n) -> p (h b) n", b=B)

        @block.sync
        def _(sp):
            sp.dma_start(ctx_raw, ctx_in.rearrange("b j d -> j b d")).then_inc(ctx_loaded, 16)
            sp.dma_start(pick[0:1, 0:NOPS], logits.rearrange("(a n) -> a n", a=1)).then_inc(small_loaded, 16)
            sp.dma_start(pick[0:1, 8:8 + NOPS], u.rearrange("(a n) -> a n", a=1)).then_inc(small_loaded, 16)
            for n in range(2):
                cols = slice(n * ID // 2, (n + 1) * ID // 2)
                sp.dma_start(wv_raw[:, :, cols], wv.rearrange("(k p) n -> p k n", p=P)[:, :, cols]).then_inc(wv_loaded[n], 16)
                if n == 0:
                    sp.dma_start(xin[:, 0, :], x[0, 0:P, :]).then_inc(x_first, 16)
            for n in range(2):
                rows = slice(n * KT // 2, (n + 1) * KT // 2)
                sp.dma_start(wq_raw[:, rows, :], wq.rearrange("(k p) n -> p k n", p=P)[:, rows, :]).then_inc(wq_loaded[n], 16)
            for n in range(2):
                rows = slice(n * HP // 2, (n + 1) * HP // 2)
                sp.dma_start(wo_raw[:, rows, :], wo.rearrange("(h p) n -> p h n", p=P)[:, rows, :]).then_inc(wo_loaded[n], 16)
            for n in range(2):
                cols = slice(n * ID // 2, (n + 1) * ID // 2)
                sp.dma_start(wk_raw[:, :, cols], wk.rearrange("(k p) n -> p k n", p=P)[:, :, cols]).then_inc(wk_loaded[n], 16)
            sp.wait_ge(idx_ready, 1)
            op = sp.value_load(pick_idx[0:1, 0:1], min_val=0, max_val=NOPS - 1)
            sp.dma_start(wf_raw, ffn_w[bass.ds(op, 1), :, :].rearrange("o (k p) n -> p (o k) n", p=P)).then_inc(wf_loaded, 16)

            def due(semaphore, count):
                sp.wait_ge(semaphore, count)
                sp.sem_inc(turn_due, 1)

            def turn_x(q1, b1):
                due(x_lo, nth(q1, b1) + 1)
                if positive(q1, b1, 1):
                    due(s_done, nth(q1, b1, len(BANKS)))
                sp.dma_start_transpose(xT.rearrange("p s k n -> p (s k) n"),
                                       xs.rearrange("p s n -> p (s n)")).then_inc(xT_turned, 16)

            def load_x(ql, bl):
                sp.wait_ge(res_ready, nth(ql, bl) - 1)
                sp.dma_start(xin[:, bl % 2, :], x[bl, bass.ds(ql * P, P), :]).then_inc(x_loaded[bl % 2], 16)

            turn_x(0, 0)
            sp.wait_ge(pads_set, 1)
            sp.wait_ge(k_done, HP)
            sp.wait_ge(wqT_done, HP)
            for t in range(KT):
                sp.wait_ge(vwT_tail, t + 1)
                sp.wait_ge(vwT_lo, (t + 1) * LOWS[HP])
                if t == 1:
                    sp.wait_ge(wo_lo, KT)
                if t == KT - 2:
                    sp.wait_ge(k_hi, 8)
                    sp.wait_ge(k_lo, 2)
                for b in range(B):
                    if (t, b) == (KT - 1, 2):
                        sp.wait_ge(vw_turned[t], 16 * b)
                        sp.dma_start(xin[:, 0, :], x[0, 0:P, :]).then_inc(x_loaded[0], 16)
                        sp.dma_start(xin[:, 1, :], x[1, 0:P, :]).then_inc(x_loaded[1], 16)
                    sp.dma_start_transpose(vw[:, t, b, :, :], slots[:, t, b, :]).then_inc(
                        vw_turned_end if t == KT - 1 and b >= 2 else vw_turned[t], 16)
            sp.wait_ge(a_done, KT * HP)
            sp.dma_start(bias[:, 0, :], bo.rearrange("(a n) -> a n", a=1).to_broadcast([P, D])).then_inc(bias_loaded, 16)
            sp.dma_start(bias[:, 1, :], ffn_b[bass.ds(op, 1), :].to_broadcast([P, D])).then_inc(bias_loaded, 16)
            for t in range(KT):
                sp.wait_ge(vw_turned[t], 16 * (B if t < KT - 1 else 2))
            sp.wait_ge(vw_turned_end, 16 * 2)

            def step(q, b):
                q1, b1 = tile(q, b, 1)
                q2, b2 = tile(q, b, -2)
                q3, b3 = tile(q, b, -3)
                ql, bl = tile(q, b, 3)

                def store():
                    sp.wait_ge(out_ready, nth(q3, b3) + 1)
                    sp.dma_start(out[b3, bass.ds(q3 * P, P), :], outb[:, b3 % 2, :]).then_inc(out_stored[b3 % 2], 16)

                if valid(q3) and valid(q):
                    store()
                if valid(q2):
                    if positive(q2, b2, 1) and not is_last(q2, b2):
                        due(f_done, nth(q2, b2))
                    due(x2_lo, nth(q2, b2) + 1)
                    turned = x2_place(q2, b2)
                    sp.dma_start_transpose(turned.rearrange("p s k n -> p (s k) n"),
                                           x2s.rearrange("p s n -> p (s n)")).then_inc(x2T_turned, 16)
                if valid(q3) and not valid(q):
                    store()
                if valid(q1):
                    turn_x(q1, b1)
                if isinstance(q, int) and (q, b) == (0, 0):
                    load_x(0, 2)
                if valid(ql):
                    load_x(ql, bl)
                if valid(q):
                    *early, last = pieces(q, b)
                    turned = probs_place(q, b)
                    if not positive(q, b, 1):
                        sp.wait_ge(pad_zeroed, 1)
                    elif not early:
                        due(o_done, nth(q, b))
                    for piece in early:
                        for s, half_ready in enumerate((p_hi, p_lo)):
                            due(half_ready, pieces_done(q, b, piece))
                            sp.dma_start_transpose(turned[:, s * NC:s * NC + EARLY, :],
                                                   ps[:, s * LOW:s * LOW + EARLY * P]).then_inc(pT_parts[s], 16)
                    due(p_tail, nth(q, b) + 1)
                    if early:
                        sp.dma_start_transpose(turned[:, EARLY:NC, :], ps[:, EARLY * P:LOW]).then_inc(pT_parts[2], 16)
                    due(p_lo, pieces_done(q, b, last))
                    start = NC + EARLY if early else 0
                    sp.dma_start_transpose(turned[:, start:, :], ps[:, start * P:]).then_inc(pT_turned, 16)

            steps(sp, step)
            for r in range(2):
                sp.wait_ge(out_stored[r], 16 * (NT // 2))

        @block.gpsimd
        def _(pool):
            nc.gpsimd.memset(ident[:, :], 0.0).then_inc(ident_zero, 1)
            pool.wait_ge(ident_zero, 1)
            nc.gpsimd.affine_select(out=ident[:, :], in_=ident[:, :], compare_op=ALU.not_equal, fill=1.0, base=0,
                                    pattern=[[-1, P]], channel_multiplier=1).then_inc(ident_ready, 1)
            pool.dma_start(gate_in[:, 0:1], g_xattn.rearrange("(a n) -> a n", a=1).to_broadcast([P, 1])).then_inc(gates_loaded, 16)
            pool.dma_start(gate_in[:, 1:2], g_ffn.rearrange("(a n) -> a n", a=1).to_broadcast([P, 1])).then_inc(gates_loaded, 16)
            nc.gpsimd.memset(neg_half, -0.5).then_inc(consts_set, 1)
            nc.gpsimd.memset(eps, EPS).then_inc(consts_set, 1)
            pool.wait_ge(consts_set, 2)

            def x_scale(q1, b1):
                pool.wait_ge(x_var, nth(q1, b1) + 1)
                nc.gpsimd.tensor_tensor(ve1, mv1[:, 1:2], eps, ALU.add).then_inc(ve1_ready, 1)
                pool.wait_ge(ve1_ready, nth(q1, b1) + 1)
                nc.gpsimd.tensor_tensor(rstd1, ve1, neg_half, ALU.pow).then_inc(x_rstd, 1)

            nc.gpsimd.memset(v_diag.rearrange("p s h b e n -> p (s h b e n)").bitcast(U32), 0).then_inc(diag_zeroed, 1)
            x_scale(0, 0)
            nc.gpsimd.memset(k_diag.rearrange("p s h b e n -> p (s h b e n)").bitcast(U32), 0).then_inc(diag_zeroed, 1)

            def share(k):
                pool.wait_ge(amax_ready, k + 1)
                nc.gpsimd.partition_all_reduce(amax_all[:, k:k + 1], amax[:, k:k + 1], P,
                                               bass.bass_isa.ReduceOp.max).then_inc(amax_shared, 1)

            def output_low(t):
                cols = slice(t * P, (t + 1) * P)
                pool.wait_ge(scale_ready, WO + 1)
                if t > 0:
                    pool.wait_ge(wo_lo, t)
                nc.gpsimd.tensor_tensor(wo_scaled, wo_raw[:, :, cols], scl[:, WO:WO + 1].unsqueeze(2).to_broadcast([P, HP, P]),
                                        ALU.mult).then_inc(wo_scaled_ready, 1)
                pool.wait_ge(wo_scaled_ready, t + 1)
                pool.wait_ge(wo_hi, t + 1)
                nc.gpsimd.tensor_tensor(wo_split[:, 1, :, cols], wo_scaled, wo_split[:, 0, :, cols],
                                        ALU.subtract).then_inc(wo_lo, 1)

            for k in (WQ, VV, WO):
                share(k)
            for t in range(KT // 2):
                output_low(t)
            share(KK)
            pool.wait_ge(v_lo, 2)
            pool.wait_ge(k_done, HP)
            pool.wait_ge(xT_turned, 16)
            nc.gpsimd.memset(slots.rearrange("p t b (s n) -> p (t b s) n", s=2)[:, :, BODY + TAIL + TH:LOW], 0.0).then_inc(pads_set, 1)
            for t in range(KT // 2, KT):
                output_low(t)
            pool.wait_ge(scale_ready, KK + 1)
            pool.wait_ge(wo_lo, KT)
            nc.gpsimd.tensor_tensor(k_scaled, kT, scl[:, KK:KK + 1].unsqueeze(2).to_broadcast([P, HP, BJ]), ALU.mult).then_inc(k_scaled_ready, 1)
            pool.wait_ge(k_scaled_ready, 1)
            for e in range(2):
                rows = slice(DH * e, DH * e + DH)
                pool.wait_ge(*((wo_lo, KT) if e == 0 else (k_lo, e)))
                pool.wait_ge(k_hi, 4 * e + 4)
                nc.gpsimd.tensor_tensor(one_head(k_diag, rows, 1, e), by_batch(k_scaled, rows), one_head(k_diag, rows, 0, e),
                                        ALU.subtract).then_inc(k_lo, 1)

            def residual(q1, b1):
                if positive(q1, b1, 4):
                    pool.wait_ge(out_ready, nth(q1, b1) - 3)
                nc.gpsimd.tensor_tensor(res[:, b1, :], xin[:, b1 % 2, :], bias[:, 0, :], ALU.add).then_inc(res_ready, 1)

            pool.wait_ge(k_lo, 2)
            x_scale(0, 1)
            pool.wait_ge(a_done, KT * HP)
            nc.gpsimd.memset(ps.rearrange("p (s n) -> p s n", s=2)[:, :, BODY + TAIL + TH:LOW], 0.0).then_inc(pad_zeroed, 1)
            pool.wait_ge(bias_loaded, 32)
            pool.wait_ge(gate_ready, 1)
            for k in range(2):
                nc.gpsimd.tensor_tensor(bias[:, k, :], bias[:, k, :], gates[:, k:k + 1].to_broadcast([P, D]), ALU.mult).then_inc(bias_ready, 1)
            pool.wait_ge(bias_ready, 2)
            pool.wait_ge(x_loaded[0], 16)
            residual(0, 0)

            def step(q, b):
                q1, b1 = tile(q, b, 1)
                q2, b2 = tile(q, b, -2)
                if valid(q2):
                    pool.wait_ge(x2_var, nth(q2, b2) + 1)
                    nc.gpsimd.tensor_tensor(ve2, mv2[:, 1:2], eps, ALU.add).then_inc(ve2_ready, 1)
                    pool.wait_ge(ve2_ready, nth(q2, b2) + 1)
                    nc.gpsimd.tensor_tensor(rstd2, ve2, neg_half, ALU.pow).then_inc(x2_rstd, 1)
                if valid(q1):
                    if not isinstance(q, int) or nth(q1, b1) > 1:
                        x_scale(q1, b1)
                    residual(q1, b1)
                if isinstance(q, int) and (q, b) == (0, 0):
                    share(WF)
                if valid(q2):
                    pool.wait_ge(x2n_ready, nth(q2, b2) + 1)
                    nc.gpsimd.tensor_tensor(res[:, b2, :], res[:, b2, :], bias[:, 1, :], ALU.add).then_inc(x2b_ready, 1)

            steps(pool, step)

        @block.scalar
        def _(act):
            for b in range(B):
                act.wait_ge(ctxT_done, b + 1)
                nc.scalar.copy(ctxT[:, :, b * J:(b + 1) * J],
                               banks[:, b, 0:CT * J].rearrange("p (k n) -> p k n", k=CT)).then_inc(ctxT_copied, 1)
            act.wait_ge(small_loaded, 32)
            act.wait_ge(pick_step, 2)
            nc.scalar.activation(pick[0:1, 24:32], pick[0:1, 16:24], ACT.Exp, accum_out=pick[0:1, 32:33]).then_inc(pick_step, 1)
            act.wait_ge(pick_step, 3)
            nc.scalar.activation(pick[0:1, 33:34], pick[0:1, 32:33], ACT.Ln).then_inc(pick_step, 1)
            nc.scalar.activation(pick[0:1, 40:48], pick[0:1, 8:16], ACT.Ln).then_inc(pick_step, 1)
            act.wait_ge(pick_step, 5)
            nc.scalar.activation(pick[0:1, 48:56], pick[0:1, 40:48], ACT.Ln, scale=-1.0).then_inc(pick_step, 1)

            def blocks_high(diag, data, k, e, h0, h1):
                rows = slice(DH * e, DH * e + DH)
                return nc.scalar.activation(diag[rows, 0, h0:h1, :, e, :].rearrange("p h b n -> p (h b) n"),
                                            data[rows, h0:h1, :].rearrange("p h (b n) -> p (h b) n", b=B),
                                            ACT.Copy, scale=scl[rows, k:k + 1])

            def x_high(q1, b1):
                act.wait_ge(xn_ready, nth(q1, b1) + 1)
                if positive(q1, b1, 1):
                    act.wait_ge(xT_turned, nth(q1, b1, 16))
                nc.scalar.activation(xs[:, 0, :], xn, ACT.Copy, scale=2.0 ** XN_BITS).then_inc(x_hi, 1)

            x_high(0, 0)

            def copy_v(h):
                act.wait_ge(v_done, h + 2)
                nc.scalar.copy(vT[:, h:h + 2, :], banks[:, h:h + 2, 0:BJ]).then_inc(v_copied, 1)

            def copy_k(h):
                act.wait_ge(k_done, h + 2)
                nc.scalar.copy(kT[:, h:h + 2, :], banks[:, h:h + 2, 0:BJ]).then_inc(k_copied, 1)

            def query_high(h):
                act.wait_ge(wqT_done, h + 1)
                nc.scalar.activation(wqT[:, 0, h, :], banks[:, h, :], ACT.Copy, scale=scl[:, WQ:WQ + 1]).then_inc(wqT_hi, 1)

            def output_high(t):
                cols = slice(t * P, (t + 1) * P)
                nc.scalar.activation(wo_split[:, 0, :, cols], wo_raw[:, :, cols], ACT.Copy, scale=scl[:, WO:WO + 1]).then_inc(wo_hi, 1)

            for h in range(0, HP, 2):
                copy_v(h)
            act.wait_ge(scale_ready, WQ + 1)
            for h in range(HP):
                query_high(h)
            act.wait_ge(scale_ready, VV + 1)
            act.wait_ge(diag_zeroed, 1)
            for e in range(2):
                blocks_high(v_diag, vT, VV, e, 0, HP).then_inc(v_hi, 1)
            act.wait_ge(scale_ready, WO + 1)
            output_high(0)
            output_high(1)
            copy_k(0)
            copy_k(2)
            output_high(2)
            copy_k(4)
            output_high(3)
            copy_k(6)

            def fold_v_high(t):
                for h in range(HP):
                    act.wait_ge(vwT_done, t * HP + (h + 1))
                    nc.scalar.activation(slot(t, slice(h * PW, (h + 1) * PW)), pair_banks(h), ACT.Copy,
                                         scale=2.0 ** FOLD_BITS).then_inc(vwT_hi, 1)
                    n = (t * HP + h - 2) // 3
                    if n < 8 and (t * HP + h - 2) % 3 == 0:
                        if n == 0:
                            act.wait_ge(scale_ready, KK + 1)
                            act.wait_ge(diag_zeroed, 2)
                        blocks_high(k_diag, kT, KK, n // 4, n % 4 * 2, n % 4 * 2 + 2).then_inc(k_hi, 1)
                act.wait_ge(vwT_hi, t * HP + HP)
                nc.scalar.copy(slot(t, slice(LOW + BODY, LOW + BODY + TAIL)), slot(t, slice(BODY, HJ))).then_inc(vwT_tail, 1)

            for t in range(KT):
                if t == KT - 1:
                    act.wait_ge(xT_turned, 16)
                fold_v_high(t)
            act.wait_ge(gates_loaded, 32)
            nc.scalar.activation(gates, gate_in, ACT.Tanh).then_inc(gate_ready, 1)

            for k in range(KT):
                act.wait_ge(vw_turned[min(k, KT - 2)], 16 * B)
                for h in range(HP):
                    act.wait_ge(a_done, k * HP + h + 1)
                    nc.scalar.activation(a_split[:, k, 0, :, h * PW:(h + 1) * PW], pair_banks(h), ACT.Copy,
                                         scale=2.0 ** FOLD_BITS).then_inc(a_hi, 1)
            act.wait_ge(exp_scale_ready, 1)

            def step(q, b):
                q1, b1 = tile(q, b, 1)
                q2, b2 = tile(q, b, -2)
                if valid(q2):
                    act.wait_ge(x2n_ready, nth(q2, b2) + 1)
                    if positive(q2, b2, 1):
                        act.wait_ge(x2T_turned, nth(q2, b2, 16))
                    nc.scalar.activation(x2s[:, 0, :], x2n, ACT.Copy, scale=2.0 ** XN_BITS).then_inc(x2_hi, 1)
                first = isinstance(q, int) and (q, b) == (0, 0)
                if first:
                    x_high(q1, b1)
                if valid(q):
                    exponentials(q, b, 0)
                if valid(q1) and not first:
                    x_high(q1, b1)
                if valid(q):
                    exponentials(q, b, 1)
                    exponentials(q, b, 2)
                    *_, last = pieces(q, b)
                    for piece in pieces(q, b):
                        probs_high(q, b, piece)
                    act.wait_ge(p_hi, pieces_done(q, b, last))
                    nc.scalar.copy(ps.rearrange("p (s n) -> p s n", s=2)[:, :, HJ:HJ + TH],
                                   ps[:, BODY:HJ].rearrange("p (s n) -> p s n", s=2)).then_inc(p_tail, 1)
                    if isinstance(q, int) and (q, b) == (0, 1):
                        act.wait_ge(scale_ready, WF + 1)
                        nc.scalar.activation(wf_split[:, 0, :, :], wf_raw, ACT.Copy, scale=scl[:, WF:WF + 1]).then_inc(wf_hi, 1)

            NB = len(BANKS)

            def exponentials(q, b, k):
                cols = slice(BANKS[k][0] * J, BANKS[k][1] * J)
                act.wait_ge(shifted, nth(q, b, NB) + k + 1)
                nc.scalar.activation(probs[:, cols], probs[:, cols], ACT.Exp, scale=exp_scale).then_inc(exp_done, 1)

            def probs_high(q, b, piece):
                h0, h1 = heads_of(piece)
                act.wait_ge(p_ready, pieces_done(q, b, piece))
                if piece[0] == 0 and positive(q, b, 1):
                    act.wait_ge(pT_turned, nth(q, b, 16))
                    if isinstance(q, int) and (q, b) == (0, 1):
                        for part_turned in pT_parts:
                            act.wait_ge(part_turned, 16)
                elif piece[0] == 0:
                    act.wait_ge(pad_zeroed, 1)
                nc.scalar.activation(ps[:, h0 * J:h1 * J], probs[:, h0 * J:h1 * J], ACT.Copy,
                                     scale=2.0 ** PROB_BITS).then_inc(p_hi, 1)

            steps(act, step)

        @block.vector
        def _(dve):
            draw_logits, shifted_logits = pick[0:1, 0:8], pick[0:1, 16:24]
            dve.wait_ge(small_loaded, 32)
            nc.vector.reduce_max(pick[0:1, 34:35], draw_logits, AX.X).then_inc(pick_step, 1)
            dve.wait_ge(pick_step, 1)
            nc.vector.tensor_scalar(shifted_logits, draw_logits, pick[0:1, 34:35], None, ALU.subtract).then_inc(pick_step, 1)
            dve.wait_ge(pick_step, 6)
            nc.vector.tensor_scalar(pick[0:1, 56:64], shifted_logits, pick[0:1, 33:34], None, ALU.subtract).then_inc(pick_step, 1)
            dve.wait_ge(pick_step, 7)
            nc.vector.tensor_tensor(pick[0:1, 64:72], pick[0:1, 56:64], pick[0:1, 48:56], ALU.subtract).then_inc(pick_step, 1)
            dve.wait_ge(pick_step, 8)
            nc.vector.max(pick[0:1, 72:80], pick[0:1, 64:72]).then_inc(pick_step, 1)
            dve.wait_ge(pick_step, 9)
            nc.vector.max_index(pick_idx[0:1, :], pick[0:1, 72:80], pick[0:1, 64:72]).then_inc(idx_ready, 1)

            def power_of_two_scale(k, bits):
                dve.wait_ge(amax_shared, k + 1)
                nc.vector.tensor_scalar(amax[:, k:k + 1], amax_all[:, k:k + 1], 1e-30, None, ALU.max).then_inc(pow2_ready, 1)
                dve.wait_ge(pow2_ready, 3 * k + 1)
                nc.vector.tensor_scalar(pow2[:, k:k + 1].bitcast(U32), amax[:, k:k + 1].bitcast(U32), 0x7F800000, None,
                                        ALU.bitwise_and).then_inc(pow2_ready, 1)
                dve.wait_ge(pow2_ready, 3 * k + 2)
                nc.vector.tensor_scalar(pow2[:, k:k + 1], pow2[:, k:k + 1], 2.0 ** -bits, None, ALU.mult).then_inc(pow2_ready, 1)
                dve.wait_ge(pow2_ready, 3 * k + 3)
                nc.vector.reciprocal(scl[:, k:k + 1], pow2[:, k:k + 1]).then_inc(scale_ready, 1)

            def part(n, data, copied, parts):
                dve.wait_ge(copied, n + 1)
                nc.vector.tensor_reduce(part_max[:, n:n + 1], data[:, 2 * n:2 * n + 2, :], AX.XY, ALU.max,
                                        apply_absolute_value=True).then_inc(parts, 1)

            def half(n, maxima, data, loaded, parts):
                dve.wait_ge(loaded[n], 16)
                rows = data.shape[1] // 2
                nc.vector.tensor_reduce(maxima[:, n:n + 1], data[:, n * rows:(n + 1) * rows, :], AX.XY, ALU.max,
                                        apply_absolute_value=True).then_inc(parts, 1)

            def largest_part(k, maxima, parts):
                dve.wait_ge(parts, maxima.shape[1])
                nc.vector.reduce_max(amax[:, k:k + 1], maxima, AX.X).then_inc(amax_ready, 1)

            def x_moments(q1, b1):
                if positive(q1, b1, 1):
                    dve.wait_ge(x_loaded[b1 % 2], (q1 * 2 + b1 // 2 + 1) * 16)
                else:
                    dve.wait_ge(x_first, 16)
                nc.vector.bn_stats(bn1, xin[:, b1 % 2, :]).then_inc(x_stats, 1)

            def x_variance():
                nc.vector.bn_aggr(mv1, bn1).then_inc(x_var, 1)

            def x_normalized(q1, b1):
                dve.wait_ge(x_rstd, nth(q1, b1) + 1)
                nc.vector.tensor_scalar(xn, xin[:, b1 % 2, :], mv1[:, 0:1], rstd1, ALU.subtract, ALU.mult).then_inc(xn_ready, 1)

            def x_low(q1, b1):
                dve.wait_ge(x_hi, nth(q1, b1) + 1)
                low(xs[:, 1, :], xn, 2.0 ** XN_BITS, xs[:, 0, :]).then_inc(x_lo, 1)

            x_moments(0, 0)
            dve.wait_ge(x_stats, 1)
            x_variance()
            x_normalized(0, 0)
            x_low(0, 0)
            part(0, vT, v_copied, v_part)
            half(0, wq_max, wq_raw, wq_loaded, wq_part)
            half(1, wq_max, wq_raw, wq_loaded, wq_part)
            largest_part(WQ, wq_max, wq_part)
            part(1, vT, v_copied, v_part)
            power_of_two_scale(WQ, OPERAND_BITS)

            def query_low(h):
                dve.wait_ge(wqT_hi, h + 1)
                low(wqT[:, 1, h, :], banks[:, h, :], scl[:, WQ:WQ + 1], wqT[:, 0, h, :]).then_inc(wqT_lo, 1)

            half(0, wo_max, wo_raw, wo_loaded, wo_part)
            part(2, vT, v_copied, v_part)
            part(3, vT, v_copied, v_part)
            largest_part(VV, part_max, v_part)
            dve.wait_ge(scale_ready, WQ + 1)
            for h in range(3):
                query_low(h)
            power_of_two_scale(VV, OPERAND_BITS)
            half(1, wo_max, wo_raw, wo_loaded, wo_part)
            largest_part(WO, wo_max, wo_part)
            query_low(3)
            query_low(4)
            power_of_two_scale(WO, OPERAND_BITS)
            for h in range(5, HP):
                query_low(h)
            back = [2.0 ** (-FOLD_BITS - XN_BITS) * DH ** -0.5, 2.0 ** (-FOLD_BITS - PROB_BITS), 2.0 ** -XN_BITS]
            dve.wait_ge(scale_ready, VV + 1)
            for e in range(2):
                rows = slice(DH * e, DH * e + DH)
                dve.wait_ge(v_hi, e + 1)
                low(one_head(v_diag, rows, 1, e), by_batch(vT, rows), scl[rows, VV:VV + 1], one_head(v_diag, rows, 0, e)).then_inc(v_lo, 1)
            for n in range(HP // 2):
                part(n, kT, k_copied, k_part)
            largest_part(KK, part_max, k_part)

            def fold_v_low(t):
                for h in range(HP):
                    dve.wait_ge(vwT_hi, t * HP + (h + 1))
                    for lo, hi, to in low_pieces(h):
                        low(slot(t, slice(to, to + hi - lo)), pair_banks(h)[:, :, lo:hi], 2.0 ** FOLD_BITS,
                            slot(t, slice(h * PW + lo, h * PW + hi))).then_inc(vwT_lo, 1)

            power_of_two_scale(KK, OPERAND_BITS)
            nc.vector.scalar_tensor_tensor(out=exp_scale, in0=pow2[:, KK:KK + 1], scalar=back[0], in1=pow2[:, WQ:WQ + 1],
                                           op0=ALU.mult, op1=ALU.mult).then_inc(exp_scale_ready, 1)
            with dve.Fori(0, KT) as t:
                fold_v_low(t)

            for k in range(KT):
                dve.wait_ge(vw_turned[min(k, KT - 2)], 16 * B)
                for h in range(HP):
                    dve.wait_ge(a_hi, k * HP + h + 1)
                    low(a_split[:, k, 1, :, h * PW:(h + 1) * PW], pair_banks(h), 2.0 ** FOLD_BITS,
                        a_split[:, k, 0, :, h * PW:(h + 1) * PW]).then_inc(a_lo, 1)


            def matrix_part(k):
                if k == 0:
                    dve.wait_ge(wf_loaded, 16)
                nc.vector.tensor_reduce(wf_max[:, k:k + 1], wf_raw[:, k, :], AX.X, ALU.max,
                                        apply_absolute_value=True).then_inc(wf_part, 1)

            def loop_scales():
                power_of_two_scale(WF, WF_BITS)
                nc.vector.scalar_tensor_tensor(out=amax[:, 7:8], in0=pow2[:, VV:VV + 1], scalar=back[1], in1=pow2[:, WO:WO + 1],
                                               op0=ALU.mult, op1=ALU.mult).then_inc(o_scale_ready, 1)
                dve.wait_ge(gate_ready, 1)
                nc.vector.scalar_tensor_tensor(out=f_scale, in0=pow2[:, WF:WF + 1], scalar=back[2], in1=gates[:, 1:2],
                                               op0=ALU.mult, op1=ALU.mult).then_inc(f_scale_ready, 1)
                dve.wait_ge(o_scale_ready, 1)
                nc.vector.tensor_tensor(o_scale, amax[:, 7:8], gates[:, 0:1], ALU.mult).then_inc(o_scale_ready, 1)

            def matrix_low():
                dve.wait_ge(wf_hi, 1)
                dve.wait_ge(scale_ready, WF + 1)
                low(wf_split[:, 1, :, :].rearrange("p k n -> p (k n)"), wf_raw.rearrange("p k n -> p (k n)"),
                    scl[:, WF:WF + 1], wf_split[:, 0, :, :].rearrange("p k n -> p (k n)")).then_inc(wf_lo, 1)

            NB = len(BANKS)

            def by_head(ap):
                return ap.rearrange("p (h n) -> p h n", n=J)

            def step(q, b):
                q1, b1 = tile(q, b, 1)
                qp, bp = tile(q, b, -1)
                q2, b2 = tile(q, b, -2)
                q3, b3 = tile(q, b, -3)

                def maxima(k):
                    h0, h1 = BANKS[k]
                    dve.wait_ge(s_done, nth(q, b, NB) + k + 1)
                    nc.vector.reduce_max(mx[:, h0:h1], by_head(s_ps[:, k, 0:(h1 - h0) * J]), AX.X).then_inc(mx_ready, 1)

                def shift(k):
                    h0, h1 = BANKS[k]
                    dve.wait_ge(mx_ready, nth(q, b, NB) + k + 1)
                    nc.vector.tensor_tensor(by_head(probs[:, h0 * J:h1 * J]), by_head(s_ps[:, k, 0:(h1 - h0) * J]),
                                            mx[:, h0:h1].unsqueeze(2).to_broadcast([P, h1 - h0, J]), ALU.subtract).then_inc(shifted, 1)

                def softmax(piece):
                    h0, h1 = heads_of(piece)
                    there = pieces_done(q, b, piece)
                    values, factors = by_head(probs[:, h0 * J:h1 * J]), rsum[:, h0:h1]
                    dve.wait_ge(exp_done, nth(q, b, NB) + piece[1])
                    nc.vector.reduce_sum(sums[:, h0:h1], values, AX.X).then_inc(sum_ready, 1)
                    dve.wait_ge(sum_ready, there)
                    nc.vector.reciprocal(factors, sums[:, h0:h1]).then_inc(rsum_ready, 1)
                    dve.wait_ge(rsum_ready, there)
                    nc.vector.tensor_tensor(values, values, factors.unsqueeze(2).to_broadcast([P, h1 - h0, J]),
                                            ALU.mult).then_inc(p_ready, 1)

                def probs_low(piece):
                    h0, h1 = heads_of(piece)
                    dve.wait_ge(p_hi, pieces_done(q, b, piece))
                    low(ps[:, LOW + h0 * J:LOW + h1 * J], probs[:, h0 * J:h1 * J], 2.0 ** PROB_BITS,
                        ps[:, h0 * J:h1 * J]).then_inc(p_lo, 1)

                def output():
                    if not positive(q3, b3, 1):
                        dve.wait_ge(f_scale_ready, 1)
                    dve.wait_ge(f_done, nth(q3, b3) + 1)
                    dve.wait_ge(x2b_ready, nth(q3, b3) + 1)
                    if positive(q3, b3, 2):
                        dve.wait_ge(out_stored[b3 % 2], (q3 * 2 + b3 // 2) * 16)
                    nc.vector.scalar_tensor_tensor(out=outb[:, b3 % 2, :], in0=f_ps, scalar=f_scale, in1=res[:, b3, :],
                                                   op0=ALU.mult, op1=ALU.add).then_inc(out_ready, 1)

                def attention_sum():
                    dve.wait_ge(o_done, nth(qp, bp) + 1)
                    dve.wait_ge(res_ready, nth(qp, bp) + 1)
                    if not positive(qp, bp, 1):
                        dve.wait_ge(o_scale_ready, 2)
                    nc.vector.scalar_tensor_tensor(out=res[:, bp, :], in0=o_ps, scalar=o_scale, in1=res[:, bp, :],
                                                   op0=ALU.mult, op1=ALU.add).then_inc(x2_ready, 1)
                    dve.wait_ge(x2_ready, nth(qp, bp) + 1)
                    nc.vector.bn_stats(bn2, res[:, bp, :]).then_inc(x2_stats, 1)

                first = isinstance(q, int) and (q, b) == (0, 0)
                second = isinstance(q, int) and (q, b) == (0, 1)
                if valid(q2):
                    dve.wait_ge(x2_stats, nth(q2, b2) + 1)
                if valid(q3) and valid(q):
                    output()
                if valid(q1):
                    x_moments(q1, b1)
                if valid(q2):
                    nc.vector.bn_aggr(mv2, bn2).then_inc(x2_var, 1)
                if valid(q1):
                    dve.wait_ge(x_stats, nth(q1, b1) + 1)
                if valid(q) and not first:
                    maxima(0)
                if valid(q1):
                    x_variance()
                if first:
                    matrix_part(0)
                    x_normalized(q1, b1)
                    matrix_part(1)
                    x_low(q1, b1)
                    maxima(0)
                if valid(q):
                    shift(0)
                if valid(q2):
                    dve.wait_ge(x2_rstd, nth(q2, b2) + 1)
                    nc.vector.tensor_scalar(x2n, res[:, b2, :], mv2[:, 0:1], rstd2, ALU.subtract, ALU.mult).then_inc(x2n_ready, 1)
                if valid(q):
                    maxima(1)
                if valid(q1) and not first:
                    x_normalized(q1, b1)
                if valid(q):
                    shift(1)
                if valid(q2):
                    dve.wait_ge(x2_hi, nth(q2, b2) + 1)
                    low(x2s[:, 1, :], x2n, 2.0 ** XN_BITS, x2s[:, 0, :]).then_inc(x2_lo, 1)
                    if not positive(q2, b2, 1):
                        matrix_low()
                if valid(q):
                    maxima(2)
                    shift(2)
                if valid(q1) and not first:
                    x_low(q1, b1)
                if valid(q):
                    *early, last = pieces(q, b)
                    for piece in early:
                        softmax(piece)
                    softmax(last)
                    between = not (first or second or early)
                    if between:
                        attention_sum()
                    for piece in pieces(q, b):
                        probs_low(piece)
                    if first:
                        matrix_part(2)
                        matrix_part(3)
                        largest_part(WF, wf_max, wf_part)
                    if second:
                        loop_scales()
                if valid(q3) and not valid(q):
                    output()
                if valid(qp) and not (valid(q) and between):
                    attention_sum()

            steps(dve, step)

        @block.tensor
        def _(pe):
            def split_products(ps, lhs, rhs, first, last):
                for n, (l, r) in enumerate(((0, 0), (0, 1), (1, 0))):
                    mm = nc.tensor.matmul(ps, lhs(l), rhs(r), start=first and n == 0, stop=last and n == 2)
                return mm

            pe.wait_ge(ident_ready, 1)
            pe.wait_ge(ctx_loaded, 16)
            for b in range(B):
                for k in range(CT):
                    mm = nc.tensor.transpose(banks[:, b, k * J:(k + 1) * J], ctx_raw[:, b, k * P:(k + 1) * P], ident[0:J, 0:J])
                mm.then_inc(ctxT_done, 1)
            pe.wait_ge(ctxT_copied, B)
            for h in range(HP):
                if h % (HP // 2) == 0:
                    pe.wait_ge(wv_loaded[h // (HP // 2)], 16)
                for k in range(CT):
                    mm = nc.tensor.matmul(banks[:, h, 0:BJ], wv_raw[:, k, h * P:(h + 1) * P], ctxT[:, k, :],
                                          start=k == 0, stop=k == CT - 1)
                mm.then_inc(v_done, 1)
            for n in range(2):
                pe.wait_ge(wq_loaded[n], 16)
            for h in range(HP):
                pe.wait_ge(v_copied, h // 2 + 1)
                for k in range(KT):
                    mm = nc.tensor.transpose(banks[:, h, k * P:(k + 1) * P], wq_raw[:, k, h * P:(h + 1) * P], ident[:, :])
                mm.then_inc(wqT_done, 1)
            for h in range(HP):
                if h % (HP // 2) == 0:
                    pe.wait_ge(wk_loaded[h // (HP // 2)], 16)
                pe.wait_ge(wqT_lo, h + 1)
                for k in range(CT):
                    mm = nc.tensor.matmul(banks[:, h, 0:BJ], wk_raw[:, k, h * P:(h + 1) * P], ctxT[:, k, :],
                                          start=k == 0, stop=k == CT - 1)
                mm.then_inc(k_done, 1)
            pe.wait_ge(v_lo, 2)
            pe.wait_ge(k_copied, HP // 2)

            def fold(t, weights, blocks, freed, done):
                for h in range(HP):
                    freed(h)
                    for g in range(2):
                        mm = split_products(half_pair(2 * h + g), lambda s: weights[:, s, h, bass.ds(t * P, P)],
                                            lambda s: half_blocks(blocks, s, h, g), True, True)
                    mm.then_inc(done, 1)

            def fold_v(t):
                def freed(h):
                    if h >= 4:
                        pe.wait_ge(vwT_lo, t * LOWS[HP] + LOWS[h - 3])
                    elif not isinstance(t, int):
                        pe.wait_ge(vwT_lo, t * LOWS[HP] + (LOWS[h + 5] - LOWS[HP]))

                pe.wait_ge(wo_lo, t + 1)
                fold(t, wo_split, v_diag, freed, vwT_done)

            fold_v(0)
            with pe.Fori(1, KT) as t:
                fold_v(t)
            pe.wait_ge(k_lo, 2)

            def fold_k(k):
                def freed(h):
                    if h >= 4:
                        pe.wait_ge(a_lo, k * HP + (h - 3))
                    elif not isinstance(k, int):
                        pe.wait_ge(a_lo, k * HP + (h + 5 - HP))
                    else:
                        pe.wait_ge(vwT_lo, (KT - 1) * LOWS[HP] + LOWS[h + 5])

                fold(k, wqT, k_diag, freed, a_done)

            fold_k(0)
            with pe.Fori(1, KT) as k:
                fold_k(k)

            def scores(q, b):
                pe.wait_ge(xT_turned, nth(q, b, 16) + 16)
                for n, (h0, h1) in enumerate(BANKS):
                    if positive(q, b, 1):
                        pe.wait_ge(shifted, nth(q, b, len(BANKS)) + n + 1 - len(BANKS))
                    else:
                        pe.wait_ge(a_lo, (KT - 1) * HP + max(-(-h1 // 2), HP // 2 + n // 2 + 1))
                    for k in range(KT):
                        mm = split_products(s_ps[:, n, 0:(h1 - h0) * J], lambda s: xT[:, s, k, :],
                                            lambda s: a_split[:, k, s, b, h0 * J:h1 * J], k == 0, k == KT - 1)
                    mm.then_inc(s_done, 1)

            def attention(q, b):
                *early, last = pieces(q, b)
                turned = probs_place(q, b)
                turns = 16 if not positive(q, b, 1) else 32
                if early:
                    for s in range(2):
                        pe.wait_ge(pT_parts[s], turns)
                else:
                    pe.wait_ge(pT_turned, nth(q, b, 16) + 16)
                if positive(q, b, 1):
                    pe.wait_ge(x2_ready, nth(q, b))
                else:
                    pe.wait_ge(a_lo, KT * HP)
                    for t in range(KT):
                        pe.wait_ge(vw_turned[t], 16 * (B if t < KT - 1 else 2))
                    pe.wait_ge(vw_turned_end, 16 * 2)
                for ch in range(NC - 1):
                    if early and ch == EARLY:
                        pe.wait_ge(pT_parts[2], turns)
                        pe.wait_ge(pT_turned, nth(q, b, 16) + 16)
                    split_products(o_ps, lambda s: turned[:, s * NC + ch, :], lambda s: vw[:, :, b, s * NC + ch, :], ch == 0, False)
                for ch in (NC - 1, 2 * NC - 1):
                    mm = nc.tensor.matmul(o_ps, turned[0:TAIL + TH, ch, :], vw[0:TAIL + TH, :, b, ch, :],
                                          start=False, stop=ch == 2 * NC - 1)
                mm.then_inc(o_done, 1)

            def ffn(q, b):
                pe.wait_ge(x2T_turned, nth(q, b, 16) + 16)
                if positive(q, b, 1):
                    pe.wait_ge(out_ready, nth(q, b))
                else:
                    pe.wait_ge(wf_lo, 1)
                turned = x2_place(q, b)
                if is_last(*tile(q, b, 1)):
                    pe.wait_ge(x2_rstd, nth(q, b) + 2)
                for k in range(KT):
                    mm = split_products(f_ps, lambda s: turned[:, s, k, :], lambda s: wf_split[:, s, k, :], k == 0, k == KT - 1)
                mm.then_inc(f_done, 1)

            def step(q, b):
                qp, bp = tile(q, b, -1)
                q2, b2 = tile(q, b, -2)
                if valid(q):
                    scores(q, b)
                if valid(qp):
                    attention(qp, bp)
                if valid(q2):
                    ffn(q2, b2)

            steps(pe, step)


_INS = ["x", "ctx_768", "g_xattn", "g_ffn", "L0_xattn_Wq", "L0_xattn_Wk", "L0_xattn_Wv", "L0_xattn_Wo", "L0_xattn_bo",
        "L0_ffn_W", "L0_ffn_b", "L0_ffn_logits", "L0_ffn_u"]


def kernel(**inputs):
    import numpy as np
    import concourse.bacc as bacc
    from concourse import mybir as mb
    from concourse.bass_utils import run_bass_kernel_spmd

    nc = bacc.Bacc("TRN2", target_bir_lowering=False, num_devices=1, dynamic_dma_scratch_size=1024)
    arrays, args = {}, []
    for name in _INS:
        a = np.ascontiguousarray(inputs[name])
        arrays[f"in_{name}"] = a
        args.append(nc.dram_tensor(f"in_{name}", a.shape, mb.dt.from_np(a.dtype), kind="ExternalInput").ap())
    shape = inputs["x"].shape
    args.append(nc.dram_tensor("out_0", shape, mb.dt.float32, kind="ExternalOutput").ap())
    flamingo_layer(nc, *args)
    r = run_bass_kernel_spmd(nc, [arrays], core_ids=[0])
    return r.results[0]["out_0"]
```
